# Optimizing a Trainium2 kernel written in Bass

```python
import numpy as np
import jax
import jax.numpy as jnp

def _softmax(x, axis=-1):
    return jax.nn.softmax(x, axis=axis)

def _gelu(x):
    return jax.nn.gelu(x, approximate=True)

def _silu(x):
    return jax.nn.silu(x)

def _sigmoid(x):
    return jax.nn.sigmoid(x)

def _layernorm(x, axis=-1, eps=1e-05):
    m = jnp.mean(x, axis=axis, keepdims=True)
    v = jnp.var(x, axis=axis, keepdims=True)
    return (x - m) / jnp.sqrt(v + eps)

def _scatter_add(tgt, idx, src, axis=0):
    return tgt.at[idx].add(src)

def _segment_sum(src, seg, n):
    return jax.ops.segment_sum(src, seg, n)
kernel_name = 'mk_adaln_d2_jaxref_r8_a44b1d'

def setup_inputs(seed: int=0):
    np.random.seed(seed)
    _w = jnp.asarray

    def _L0_attn_setup():
        import jax, jax.numpy as jnp
        import numpy as np
        D_MODEL = 128
        D_STATE = 16
        D_CONV = 4
        D_INNER = 256
        BATCH = 2
        LENGTH = 256

        def silu(u):
            return u * jax.nn.sigmoid(u)
        key = jax.random.key(seed)
        ks = jax.random.split(key, 8)
        sc = 0.02
        x = jax.random.normal(ks[0], (BATCH, LENGTH, D_MODEL), jnp.float32)
        W_in = jax.random.normal(ks[1], (2 * D_INNER, D_MODEL), jnp.float32) * sc
        conv_w = jax.random.normal(ks[2], (D_INNER, 1, D_CONV), jnp.float32) * 0.1
        conv_b = jnp.zeros((D_INNER,), jnp.float32)
        W_x = jax.random.normal(ks[3], (D_INNER + 2 * D_STATE, D_INNER), jnp.float32) * sc
        W_dt = jax.random.normal(ks[4], (D_INNER, D_INNER), jnp.float32) * sc
        b_dt = jnp.zeros((D_INNER,), jnp.float32)
        A_log = jnp.log(jnp.tile(jnp.arange(1, D_STATE + 1, dtype=jnp.float32), (D_INNER, 1)))
        D = jnp.ones((D_INNER,), jnp.float32)
        W_out = jax.random.normal(ks[5], (D_MODEL, D_INNER), jnp.float32) * sc
        ln_g = jnp.ones((D_MODEL,), jnp.float32)
        ln_b = jnp.zeros((D_MODEL,), jnp.float32)
        return dict(x=x, W_in=W_in, conv_w=conv_w, conv_b=conv_b, W_x=W_x, W_dt=W_dt, b_dt=b_dt, A_log=A_log, D=D, W_out=W_out, ln_g=ln_g, ln_b=ln_b)
    _L0_attn_in = _L0_attn_setup()

    def _L0_ffn_setup():
        import jax, jax.numpy as jnp
        import numpy as np
        D_IN, D_HID = (128, 512)

        def _ternary(key, shape):
            return jax.random.randint(key, shape, -1, 2).astype(jnp.float32)

        def _tlin(x, w, s):
            return jnp.einsum('bsi,oi->bso', x, w) * s
        key = jax.random.key(seed)
        ks = jax.random.split(key, 12)
        inv = lambda fan: 1.0 / np.sqrt(fan).astype(np.float32)
        return {'x': jax.random.normal(ks[0], (4, 256, D_IN), dtype=jnp.float32), 'w1_w': _ternary(ks[1], (D_HID, D_IN)), 'w1_s': jax.random.uniform(ks[2], (D_HID,), dtype=jnp.float32) * inv(D_IN), 'w2_w': _ternary(ks[3], (D_HID, D_IN)), 'w2_s': jax.random.uniform(ks[4], (D_HID,), dtype=jnp.float32) * inv(D_IN), 'h1_w': _ternary(ks[5], (D_HID, D_HID)), 'h1_s': jax.random.uniform(ks[6], (D_HID,), dtype=jnp.float32) * inv(D_HID), 'h2_w': _ternary(ks[7], (D_HID, D_HID)), 'h2_s': jax.random.uniform(ks[8], (D_HID,), dtype=jnp.float32) * inv(D_HID), 'w3_w': _ternary(ks[9], (D_IN, D_HID)), 'w3_s': jax.random.uniform(ks[10], (D_IN,), dtype=jnp.float32) * inv(D_HID)}
    _L0_ffn_in = _L0_ffn_setup()
    _L0_c = _w((lambda *s: np.random.randn(*s).astype(np.float32) * 0.05)(8, 128))
    _L0_wmod = _w((lambda *s: np.random.randn(*s).astype(np.float32) * 0.05)(128, 6 * 128) * 128 ** (-0.5))

    def _L1_attn_setup():
        import jax, jax.numpy as jnp
        import numpy as np
        B, S, IN_DIM, HID, H, CS = (4, 512, 128, 128, 16, 16)
        HD = HID // H
        LN_EPS = 1e-05

        def _chunk_scan(a, b):
            Bsz, Sl = (a.shape[0], a.shape[1])
            N = Sl // CS
            ac = a.reshape(Bsz, N, CS, H)
            bc = b.reshape(Bsz, N, CS, H, HD)
            cum = jnp.cumprod(ac, axis=2)
            ones = jnp.ones((Bsz, N, 1, H), a.dtype)
            cum_pad = jnp.concatenate([ones, cum[:, :, :-1]], axis=2)
            Mi = cum[:, :, :, None, :]
            Mj = cum_pad[:, :, None, :, :]
            M = jnp.where(jnp.abs(Mj) > 1e-08, Mi / Mj, jnp.zeros_like(Mi))
            tril = jnp.tril(jnp.ones((CS, CS), a.dtype))[None, None, :, :, None]
            eye = jnp.eye(CS, dtype=a.dtype)[None, None, :, :, None]
            M = M * tril
            M = M * (1 - eye) + eye
            h_contrib = jnp.einsum('bnijh,bnjhd->bnihd', M, bc)
            cum_T = jnp.moveaxis(cum, 1, 0)
            hc_T = jnp.moveaxis(h_contrib, 1, 0)

            def step(h, inp):
                cum_n, hc_n = inp
                h_chunk = cum_n[..., None] * h[:, None] + hc_n
                return (h_chunk[:, -1], h_chunk)
            h0 = jnp.zeros((Bsz, H, HD), a.dtype)
            _, h_all = jax.lax.scan(step, h0, (cum_T, hc_T))
            h_all = jnp.moveaxis(h_all, 0, 1).reshape(Bsz, Sl, HID)
            return h_all

        def _reference_tuple_inner(x, W_in, ln_g, ln_b, W_gate, b_gate, eig_raw, W_out):
            Bsz, Sl, _ = x.shape
            xp = x @ W_in.T
            mu = jnp.mean(xp, axis=-1, keepdims=True)
            var = jnp.mean((xp - mu) ** 2, axis=-1, keepdims=True)
            xp = (xp - mu) * jax.lax.rsqrt(var + LN_EPS) * ln_g + ln_b
            gates = xp @ W_gate.T + b_gate
            alpha = jax.nn.sigmoid(gates[..., :H])
            beta = jax.nn.sigmoid(gates[..., H:])
            eig = jnp.tanh(eig_raw)
            a = eig[None, None, :] * alpha
            x_heads = xp.reshape(Bsz, Sl, H, HD)
            b = beta[..., None] * x_heads
            h_all = _chunk_scan(a, b)
            output = h_all @ W_out.T
            h_final = h_all[:, -1, :]
            return (output, h_final)
        key = jax.random.key(seed)
        ks = jax.random.split(key, 6)
        x = jax.random.normal(ks[0], (B, S, IN_DIM), jnp.float32)
        W_in = jax.random.normal(ks[1], (HID, IN_DIM), jnp.float32) * IN_DIM ** (-0.5)
        ln_g = jnp.ones((HID,), jnp.float32)
        ln_b = jnp.zeros((HID,), jnp.float32)
        W_gate = jax.random.normal(ks[2], (2 * H, HID), jnp.float32) * HID ** (-0.5)
        b_gate = jnp.zeros((2 * H,), jnp.float32)
        raw = 0.5 * float(np.log(1.9 / 0.1))
        eig_raw = jnp.full((H,), raw, jnp.float32) + 0.01 * jax.random.normal(ks[3], (H,), jnp.float32)
        W_out = jax.random.normal(ks[4], (HID, HID), jnp.float32) * HID ** (-0.5)
        return {'x': x, 'W_in': W_in, 'ln_g': ln_g, 'ln_b': ln_b, 'W_gate': W_gate, 'b_gate': b_gate, 'eig_raw': eig_raw, 'W_out': W_out}
    _L1_attn_in = _L1_attn_setup()

    def _L1_ffn_setup():
        import jax, jax.numpy as jnp
        import numpy as np
        E = 8
        K = 2
        R = 64
        ALPHA = 128.0
        SCALING = ALPHA / R
        key = jax.random.key(seed)
        k0, k1, k2, k3 = jax.random.split(key, 4)
        B, S, D = (4, 512, 128)
        x = jax.random.normal(k0, (B, S, D), jnp.float32)
        Wg = jax.random.normal(k1, (E, D), jnp.float32) * 0.02
        bg = jnp.zeros((E,), jnp.float32)
        W1 = jax.random.normal(k2, (E, R, D), jnp.float32) * (1.0 / np.sqrt(D))
        W2 = jax.random.normal(k3, (E, D, R), jnp.float32) * 0.02
        return {'x': x, 'Wg': Wg, 'bg': bg, 'W1': W1, 'W2': W2}
    _L1_ffn_in = _L1_ffn_setup()
    _L1_c = _w((lambda *s: np.random.randn(*s).astype(np.float32) * 0.05)(8, 128))
    _L1_wmod = _w((lambda *s: np.random.randn(*s).astype(np.float32) * 0.05)(128, 6 * 128) * 128 ** (-0.5))
    _d = {'L0_attn_x': _L0_attn_in['x'], 'L0_attn_W_in': _L0_attn_in['W_in'], 'L0_attn_conv_w': _L0_attn_in['conv_w'], 'L0_attn_conv_b': _L0_attn_in['conv_b'], 'L0_attn_W_x': _L0_attn_in['W_x'], 'L0_attn_W_dt': _L0_attn_in['W_dt'], 'L0_attn_b_dt': _L0_attn_in['b_dt'], 'L0_attn_A_log': _L0_attn_in['A_log'], 'L0_attn_D': _L0_attn_in['D'], 'L0_attn_W_out': _L0_attn_in['W_out'], 'L0_attn_ln_g': _L0_attn_in['ln_g'], 'L0_attn_ln_b': _L0_attn_in['ln_b'], 'L0_ffn_w1_w': _L0_ffn_in['w1_w'], 'L0_ffn_w1_s': _L0_ffn_in['w1_s'], 'L0_ffn_w2_w': _L0_ffn_in['w2_w'], 'L0_ffn_w2_s': _L0_ffn_in['w2_s'], 'L0_ffn_h1_w': _L0_ffn_in['h1_w'], 'L0_ffn_h1_s': _L0_ffn_in['h1_s'], 'L0_ffn_h2_w': _L0_ffn_in['h2_w'], 'L0_ffn_h2_s': _L0_ffn_in['h2_s'], 'L0_ffn_w3_w': _L0_ffn_in['w3_w'], 'L0_ffn_w3_s': _L0_ffn_in['w3_s'], 'L0_c': _L0_c, 'L0_wmod': _L0_wmod, 'L1_attn_W_in': _L1_attn_in['W_in'], 'L1_attn_ln_g': _L1_attn_in['ln_g'], 'L1_attn_ln_b': _L1_attn_in['ln_b'], 'L1_attn_W_gate': _L1_attn_in['W_gate'], 'L1_attn_b_gate': _L1_attn_in['b_gate'], 'L1_attn_eig_raw': _L1_attn_in['eig_raw'], 'L1_attn_W_out': _L1_attn_in['W_out'], 'L1_ffn_Wg': _L1_ffn_in['Wg'], 'L1_ffn_bg': _L1_ffn_in['bg'], 'L1_ffn_W1': _L1_ffn_in['W1'], 'L1_ffn_W2': _L1_ffn_in['W2'], 'L1_c': _L1_c, 'L1_wmod': _L1_wmod}
    _x0 = _d['L0_attn_x']
    _d['L0_attn_x'] = jax.random.normal(jax.random.fold_in(jax.random.key(seed), 1), (8, 1024, 128), dtype=_x0.dtype)
    del _x0
    return _d

def reference(L0_attn_x, L0_attn_W_in, L0_attn_conv_w, L0_attn_conv_b, L0_attn_W_x, L0_attn_W_dt, L0_attn_b_dt, L0_attn_A_log, L0_attn_D, L0_attn_W_out, L0_attn_ln_g, L0_attn_ln_b, L0_ffn_w1_w, L0_ffn_w1_s, L0_ffn_w2_w, L0_ffn_w2_s, L0_ffn_h1_w, L0_ffn_h1_s, L0_ffn_h2_w, L0_ffn_h2_s, L0_ffn_w3_w, L0_ffn_w3_s, L0_c, L0_wmod, L1_attn_W_in, L1_attn_ln_g, L1_attn_ln_b, L1_attn_W_gate, L1_attn_b_gate, L1_attn_eig_raw, L1_attn_W_out, L1_ffn_Wg, L1_ffn_bg, L1_ffn_W1, L1_ffn_W2, L1_c, L1_wmod):

    def _L0_attn_ref(x, W_in, conv_w, conv_b, W_x, W_dt, b_dt, A_log, D, W_out, ln_g, ln_b):
        import jax, jax.numpy as jnp
        import numpy as np
        D_MODEL = 128
        D_STATE = 16
        D_CONV = 4
        D_INNER = 256
        BATCH = 2
        LENGTH = 256

        def silu(u):
            return u * jax.nn.sigmoid(u)
        b, l, _ = x.shape
        residual = x
        xz = x @ W_in.T
        xs, z = jnp.split(xz, 2, axis=-1)
        xc = jnp.transpose(xs, (0, 2, 1))
        xc = jax.lax.conv_general_dilated(xc, conv_w, window_strides=(1,), padding=[(D_CONV - 1, 0)], dimension_numbers=('NCH', 'OIH', 'NCH'), feature_group_count=D_INNER)
        xc = xc + conv_b[None, :, None]
        u = silu(jnp.transpose(xc, (0, 2, 1)))
        proj = u @ W_x.T
        d_in, Bm, Cm = jnp.split(proj, [D_INNER, D_INNER + D_STATE], axis=-1)
        delta = jax.nn.softplus(d_in @ W_dt.T + b_dt)
        A = -jnp.exp(A_log)
        dA = jnp.exp(delta[..., None] * A)
        dBu = delta[..., None] * Bm[:, :, None, :] * u[..., None]

        def step(state, inp):
            dA_t, dBu_t, c_t = inp
            state = state * dA_t + dBu_t
            y_t = jnp.einsum('bdn,bn->bd', state, c_t)
            return (state, y_t)
        init = jnp.zeros((b, D_INNER, D_STATE), x.dtype)
        _, ys = jax.lax.scan(step, init, (jnp.transpose(dA, (1, 0, 2, 3)), jnp.transpose(dBu, (1, 0, 2, 3)), jnp.transpose(Cm, (1, 0, 2))))
        y = jnp.transpose(ys, (1, 0, 2)) + u * D
        y = y * silu(z)
        out = y @ W_out.T + residual
        mu = jnp.mean(out, axis=-1, keepdims=True)
        var = jnp.var(out, axis=-1, keepdims=True)
        return (out - mu) / jnp.sqrt(var + 1e-05) * ln_g + ln_b

    def _L0_ffn_ref(x, w1_w, w1_s, w2_w, w2_s, h1_w, h1_s, h2_w, h2_s, w3_w, w3_s):
        import jax, jax.numpy as jnp
        import numpy as np
        D_IN, D_HID = (128, 512)

        def _ternary(key, shape):
            return jax.random.randint(key, shape, -1, 2).astype(jnp.float32)

        def _tlin(x, w, s):
            return jnp.einsum('bsi,oi->bso', x, w) * s
        h = jax.nn.silu(_tlin(x, w1_w, w1_s)) * _tlin(x, w2_w, w2_s)
        h = jax.nn.gelu(_tlin(h, h1_w, h1_s), approximate=False)
        h = jax.nn.gelu(_tlin(h, h2_w, h2_s), approximate=False)
        return _tlin(h, w3_w, w3_s)

    def _L1_attn_ref(x, W_in, ln_g, ln_b, W_gate, b_gate, eig_raw, W_out):
        import jax, jax.numpy as jnp
        import numpy as np
        B, S, IN_DIM, HID, H, CS = (4, 512, 128, 128, 16, 16)
        HD = HID // H
        LN_EPS = 1e-05

        def _chunk_scan(a, b):
            Bsz, Sl = (a.shape[0], a.shape[1])
            N = Sl // CS
            ac = a.reshape(Bsz, N, CS, H)
            bc = b.reshape(Bsz, N, CS, H, HD)
            cum = jnp.cumprod(ac, axis=2)
            ones = jnp.ones((Bsz, N, 1, H), a.dtype)
            cum_pad = jnp.concatenate([ones, cum[:, :, :-1]], axis=2)
            Mi = cum[:, :, :, None, :]
            Mj = cum_pad[:, :, None, :, :]
            M = jnp.where(jnp.abs(Mj) > 1e-08, Mi / Mj, jnp.zeros_like(Mi))
            tril = jnp.tril(jnp.ones((CS, CS), a.dtype))[None, None, :, :, None]
            eye = jnp.eye(CS, dtype=a.dtype)[None, None, :, :, None]
            M = M * tril
            M = M * (1 - eye) + eye
            h_contrib = jnp.einsum('bnijh,bnjhd->bnihd', M, bc)
            cum_T = jnp.moveaxis(cum, 1, 0)
            hc_T = jnp.moveaxis(h_contrib, 1, 0)

            def step(h, inp):
                cum_n, hc_n = inp
                h_chunk = cum_n[..., None] * h[:, None] + hc_n
                return (h_chunk[:, -1], h_chunk)
            h0 = jnp.zeros((Bsz, H, HD), a.dtype)
            _, h_all = jax.lax.scan(step, h0, (cum_T, hc_T))
            h_all = jnp.moveaxis(h_all, 0, 1).reshape(Bsz, Sl, HID)
            return h_all

        def _reference_tuple_inner(x, W_in, ln_g, ln_b, W_gate, b_gate, eig_raw, W_out):
            Bsz, Sl, _ = x.shape
            xp = x @ W_in.T
            mu = jnp.mean(xp, axis=-1, keepdims=True)
            var = jnp.mean((xp - mu) ** 2, axis=-1, keepdims=True)
            xp = (xp - mu) * jax.lax.rsqrt(var + LN_EPS) * ln_g + ln_b
            gates = xp @ W_gate.T + b_gate
            alpha = jax.nn.sigmoid(gates[..., :H])
            beta = jax.nn.sigmoid(gates[..., H:])
            eig = jnp.tanh(eig_raw)
            a = eig[None, None, :] * alpha
            x_heads = xp.reshape(Bsz, Sl, H, HD)
            b = beta[..., None] * x_heads
            h_all = _chunk_scan(a, b)
            output = h_all @ W_out.T
            h_final = h_all[:, -1, :]
            return (output, h_final)
        return _reference_tuple_inner(x, W_in, ln_g, ln_b, W_gate, b_gate, eig_raw, W_out)[0]

    def _L1_ffn_ref(x, Wg, bg, W1, W2):
        import jax, jax.numpy as jnp
        import numpy as np
        E = 8
        K = 2
        R = 64
        ALPHA = 128.0
        SCALING = ALPHA / R
        orig_shape = x.shape
        D = orig_shape[-1]
        xf = x.reshape(-1, D)
        logits = xf @ Wg.T + bg
        top_gates, top_idx = jax.lax.top_k(logits, K)
        top_gates = jax.nn.softmax(top_gates, axis=-1)
        h = jax.nn.gelu(jnp.einsum('nd,erd->enr', xf, W1), approximate=False)
        eout = SCALING * jnp.einsum('enr,edr->ned', h, W2)
        sel = jnp.take_along_axis(eout, top_idx[:, :, None], axis=1)
        out = jnp.sum(top_gates[:, :, None] * sel, axis=1)
        return out.reshape(orig_shape)
    x = L0_attn_x
    mod = (_silu(L0_c) @ L0_wmod).reshape(L0_c.shape[0], 6, 1, -1)
    sa, ca, ga, sb, cb, gb = (mod[:, 0], mod[:, 1], mod[:, 2], mod[:, 3], mod[:, 4], mod[:, 5])
    ga = (2 * (ga >= 0) - 1) * jnp.maximum(jnp.abs(ga), 0.25)
    gb = (2 * (gb >= 0) - 1) * jnp.maximum(jnp.abs(gb), 0.25)
    h = _layernorm(x, axis=-1) * (1 + ca) + sa
    x = x + ga * _L0_attn_ref(h, L0_attn_W_in, L0_attn_conv_w, L0_attn_conv_b, L0_attn_W_x, L0_attn_W_dt, L0_attn_b_dt, L0_attn_A_log, L0_attn_D, L0_attn_W_out, L0_attn_ln_g, L0_attn_ln_b)
    h = _layernorm(x, axis=-1) * (1 + cb) + sb
    x = x + gb * _L0_ffn_ref(h, L0_ffn_w1_w, L0_ffn_w1_s, L0_ffn_w2_w, L0_ffn_w2_s, L0_ffn_h1_w, L0_ffn_h1_s, L0_ffn_h2_w, L0_ffn_h2_s, L0_ffn_w3_w, L0_ffn_w3_s)
    mod = (_silu(L1_c) @ L1_wmod).reshape(L1_c.shape[0], 6, 1, -1)
    sa, ca, ga, sb, cb, gb = (mod[:, 0], mod[:, 1], mod[:, 2], mod[:, 3], mod[:, 4], mod[:, 5])
    ga = (2 * (ga >= 0) - 1) * jnp.maximum(jnp.abs(ga), 0.25)
    gb = (2 * (gb >= 0) - 1) * jnp.maximum(jnp.abs(gb), 0.25)
    h = _layernorm(x, axis=-1) * (1 + ca) + sa
    x = x + ga * _L1_attn_ref(h, L1_attn_W_in, L1_attn_ln_g, L1_attn_ln_b, L1_attn_W_gate, L1_attn_b_gate, L1_attn_eig_raw, L1_attn_W_out)
    h = _layernorm(x, axis=-1) * (1 + cb) + sb
    x = x + gb * _L1_ffn_ref(h, L1_ffn_Wg, L1_ffn_bg, L1_ffn_W1, L1_ffn_W2)
    return x

_drawn_inputs = setup_inputs


def setup_inputs(seed=0):
    import zlib

    import numpy as np

    out = dict(_drawn_inputs(seed))
    spreads = {'L0_attn_conv_b': (0.0, 0.1),
     'L0_attn_b_dt': (0.0, 0.1),
     'L0_attn_D': (1.0, 0.2),
     'L0_attn_ln_g': (1.0, 0.2),
     'L0_attn_ln_b': (0.0, 0.1),
     'L1_attn_ln_g': (1.0, 0.2),
     'L1_attn_ln_b': (0.0, 0.1),
     'L1_attn_b_gate': (0.0, 0.1),
     'L1_ffn_bg': (0.0, 0.1)}
    factors = {}
    for name, (base, spread) in spreads.items():
        noise = np.random.default_rng([zlib.crc32(name.encode()), seed]).standard_normal(out[name].shape)
        drawn = base * np.exp(spread * noise) if base else spread * noise
        out[name] = jnp.asarray(drawn.astype(out[name].dtype))
    for name, factor in factors.items():
        out[name] = (out[name] * factor).astype(out[name].dtype)
    return out
```

```python
from contextlib import ExitStack

import concourse.bass as bass
from concourse import mybir

F32 = mybir.dt.float32
BF16 = mybir.dt.bfloat16
U32 = mybir.dt.uint32
ALU = mybir.AluOpType
ACT = mybir.ActivationFunctionType

P = 128
BATCH, L = 8, 1024
NT = L // P
HALF = 512
TH = HALF // P
DI = 256
ND = DI // P
NS = 16
TAPS = 4
HID = 512
NM = HID // P
EXPERTS, RANK = 8, 64
CHUNK = 16
HEADS = 16
EPS = 1e-5
SPLIT = 3

W_PARTS = [("w_in", 2 * DI), ("w_bc", ND * 2 * NS), ("w_out", ND * P), ("w1", HID), ("w2", HID), ("h1", NM * HID),
           ("h2", NM * HID), ("w3", NM * P), ("b_in", P), ("b_gate", 2 * P), ("b_out", P), ("e1", HID),
           ("e2", NM * P), ("e_gate", EXPERTS)]
W_AT, W_COLS = {}, 0
for _name, _n in W_PARTS:
    W_AT[_name] = W_COLS
    W_COLS += _n
V_PARTS = [("conv_w", ND * TAPS), ("conv_b", ND), ("b_dt", ND), ("a_log", ND * NS), ("d", ND), ("ln_g", 1),
           ("ln_b", 1), ("w1_s", NM), ("w2_s", NM), ("h1_s", NM), ("h2_s", NM), ("w3_s", 1), ("l_g", 1), ("l_b", 1),
           ("gate_b", 2), ("eig", 1), ("bg", EXPERTS)]
V_AT, V_COLS = {}, 0
for _name, _n in V_PARTS:
    V_AT[_name] = V_COLS
    V_COLS += _n
(SA0, CA0, G_LN, G_LB, SB0, CB0, G_FFN, SA1, CA1, G_ATT, SB1, CB1, G_MOE) = range(13)
NVEC = 13


def rest_stages():
    out = [("norm", 1)]
    for h in range(2):
        out += [("gated", h, m) for m in range(NM)]
        out += [("hidden1", h, m) for m in range(NM)]
        out += [("hidden2", h, m) for m in range(NM)]
        out += [("down", h)]
    out += [("norm", 2), ("proj",), ("gates",), ("recur",), ("att_out",), ("norm", 4), ("route",)]
    for h in range(2):
        out += [("expert", h, m) for m in range(NM)]
        out += [("combine", h)]
    return out


TICKS = range(-6, 2 * NS)


def rest_plan(overlap):
    stages = rest_stages()
    plan = {t: [] for t in TICKS}
    for i, stage in enumerate(stages):
        plan[TICKS[-1]].append(stage)
    return plan


def bank_plan(do_scan, do_rest, plan):
    uses = []
    both = [(d, h) for d in range(ND) for h in range(2)]
    if do_rest:
        uses += [("rows0", "wog", 1), ("rows1", "w2g", 1), (("mix", 0), "r_norm", 4), (("mix", 1), "r_norm", 8)]
    if do_scan:
        uses += [(("in_t", h), "hcm", h + 1) for h in range(2)]
        uses += [(("xs", d, h), "xs_sb", 2 * d + h + 1) for d, h in both]
        uses += [(("z", d, h), "z", 2 * d + h + 1) for d, h in both]
        uses += [(("dt", d, h), "abs_dt", 2 * d + h + 1) for d, h in both]
        uses += [("bc", "c_sb", 1), (("b_t", 0), "b_sb", 1), (("b_t", 1), "b_sb", 2)]
    for t in TICKS if do_rest else ():
        for stage in plan[t]:
            kind, *at = stage
            h = at[0] if at else 0
            i = NM * h + at[1] + 1 if len(at) == 2 else 0
            uses += {
                "norm": [(("norm_t", h, x), "hc", {1: 0, 2: 2, 4: 4}.get(h, 0) + x + 1) for x in range(2)],
                "gated": [(("gated_a", *at), "gate_a", i), (("gated_b", *at), "h0", i)],
                "hidden1": [(stage, "g1", i)],
                "hidden2": [(stage, "g2", i)],
                "down": [(stage, "x_upd", 2 + h)],
                "proj": [(("proj", x), "r_norm", 24 + 4 * (x + 1)) for x in range(2)]
                + [(("norm_t", 3, x), "xpc", x + 1) for x in range(2)],
                "gates": [((part, x), sem, x + 1) for x in range(2)
                          for part, sem in (("alpha", "tanh_a"), ("beta", "tanh_b"))],
                "recur": [],
                "att_out": [(("att_out", x), "x_upd", 4 + x) for x in range(2)],
                "route": [("logits", "lg", 1), (("g_t", 0), "gs", 1), (("g_t", 1), "gs", 2)],
                "expert": [(("exp_h", *at), "exp_g", i), (("exp_g", *at), "gx", i)],
                "combine": [(stage, "x_upd", 6 + h)],
            }[kind]
    if do_scan:
        uses += [(("y_t", d, h), "y_sum", 2 * d + h + 1) for d, h in both]
    return {name: (i % 3, i // 3, *(uses[i - 3][1:] if i >= 3 else (None, 0))) for i, (name, _, _) in enumerate(uses)}


SEMS = """x_in cur cur_r rest_x_in diag rows w3g wog w2g stored
p_stat p_aggr p_var p_rstd p_norm hcm pad xs_sb conv u z relu_dt abs_dt exp_dt ln_dt delta du bc_split b_sb c_sb
b_full b_spread da dbu h_done ht_full acc y_sum y
r_stat r_aggr r_var r_rstd r_norm on_g x_g2 x_upd hc gate_a h0 g1 g2
tanh_a tanh_b alpha a_shift cp cp_abs b_in bg_in c_in c_last q aq hout xpc xph q0
lg top idx gap tg wts one g_split gs exp_g gx""".split()


def build(nc, x, wts, vecs, pre, cmod, wmod, out):
    with ExitStack() as ctx:
        def sb(name, shape, dt=F32):
            return ctx.enter_context(nc.sbuf_tensor(name, shape, dt))

        def ps(name, shape):
            return ctx.enter_context(nc.psum_tensor(name, shape, F32))

        s = {n: ctx.enter_context(nc.semaphore("s_" + n)) for n in SEMS}
        bank_full = [ctx.enter_context(nc.semaphore(f"bank_full{i}")) for i in range(3)]
        pre_sem = [ctx.enter_context(nc.semaphore(f"pre{i}")) for i in range(5)]
        clear = list(s.values()) + bank_full

        W = sb("W", [P, W_COLS])
        V = sb("V", [P, V_COLS])
        ident = sb("ident", [P, P])
        ones = sb("ones", [P, P])
        mhalf = sb("mhalf", [P, NT])
        iota_e = sb("iota_e", [P, EXPERTS])
        starts = sb("starts", [P, L])
        sel_b = sb("sel_b", [SPLIT * NS, NS, P], BF16)
        sel_g = sb("sel_g", [SPLIT * EXPERTS, EXPERTS, RANK], BF16)
        w_dtx = sb("w_dtx", [P, ND, DI])
        neg_a = sb("neg_a", [P, ND, NS])
        vec = sb("vec", [P, BATCH, NVEC])
        eig_half = sb("eig_half", [P, 1])
        gate_bh = sb("gate_bh", [P, 2])
        small = sb("small", [P, 256])

        cur = sb("cur", [P, NVEC])
        cur_r = sb("cur_r", [P, NVEC])
        stat = sb("stat", [P, NT, 6])
        aggr = sb("aggr", [P, NT, 2])
        rstd = sb("rstd", [P, NT])
        var = sb("var", [P, NT])
        u = sb("u", [P, ND, L])
        zs = sb("zs", [P, ND, L])
        delta = sb("delta", [P, ND, L])
        du = sb("du", [P, ND, L])
        c_tok = sb("c_tok", [P, NT, NS])
        b_tok = sb("b_tok", [P, NT, SPLIT * NS])
        b_hi = sb("b_hi", [P, 2, NT, NS], BF16)
        b_sb = sb("b_sb", [SPLIT * NS, L], BF16)
        b_spread = sb("b_spread", [P, 2, L])
        da = sb("da", [P, 4, L])
        dbu = sb("dbu", [P, 4, L])
        hst = sb("hst", [P, 4, L])
        acc = sb("acc", [P, NT, DI])
        ycm = sb("ycm", [P, ND + 1, L])
        xpad = hst[:, :, :].rearrange("p a b -> p (a b)")[:, 0:2 * (L + 4)].rearrange("p (d t) -> p d t", d=2)
        soft = dbu[:, 0:2, :]
        xt = dbu[:, 2, :].rearrange("p (j c) -> p j c", c=P)
        xn = dbu[:, 3, :].rearrange("p (j c) -> p j c", c=P)

        xr = sb("xr", [P, NT, P])
        rn = sb("rn", [P, NT, P])
        rstat = sb("rstat", [P, NT, 6])
        raggr = sb("raggr", [P, NT, 2])
        rrstd = sb("rrstd", [P, NT])
        rvar = sb("rvar", [P, NT])
        hc = sb("hc", [P, L])
        rows = sb("rows", [P, 2, P])
        w3g = sb("w3g", [P, NM, P])
        wog = sb("wog", [P, P])
        w2g = sb("w2g", [P, NM, P])
        ga = sb("ga", [P, HALF])
        hid = sb("hid", [P, 4, L])
        h0 = hid[:, 0:2, :].rearrange("p a (m t) -> p (a m) t", t=HALF)
        g1 = hid[:, 2:4, :].rearrange("p a (m t) -> p (a m) t", t=HALF)
        g2 = h0
        diag = hid[:, 3, 0:5 * P].rearrange("p (i c) -> p i c", c=P)
        rec = sb("rec", [P, L])
        xpc, al, ash, bb = hid[:, 0, :], hid[:, 1, :], hid[:, 2, :], hid[:, 3, :]
        qs = sb("qs", [P, L + 1])
        lg = sb("lg", [P, NT, EXPERTS])
        top = sb("top", [P, NT, 8])
        idx = sb("idx", [P, NT, 8], U32)
        idf = sb("idf", [P, NT, 8])
        gap = sb("gap", [P, NT, 2])
        oh = sb("oh", [P, 2, NT, EXPERTS])
        g_tok = sb("g_tok", [P, NT, SPLIT * EXPERTS])
        g_hi = sb("g_hi", [P, 2, NT, EXPERTS], BF16)
        g_sb = sb("g_sb", [SPLIT * EXPERTS, L], BF16)

        ht = [ps(f"ht{i}", [P, TH, DI]) for i in range(2)]
        bspr = ps("bspr", [P, HALF])
        bank = [ps(f"bank{i}", [P, HALF]) for i in range(3)]

        def w(name, n, at=0):
            return W[:, W_AT[name] + at:W_AT[name] + at + n]

        def v(name, i=0, n=1):
            return V[:, V_AT[name] + i:V_AT[name] + i + n]

        def half(ap, h):
            return ap[:, h * HALF:(h + 1) * HALF]

        ld, pv, pp, pa, pt = pre_sem
        wx = da[:, 0:2, :].rearrange("p a b -> p (a b)")[:, 0:2 * ND * DI].rearrange("p (a j k) -> p a j k", a=2, j=ND)
        cm = small[:, 0:2 * BATCH]
        cms = small[:, 16:16 + 2 * BATCH]
        wm = hst[:, 0:2, :].rearrange("p a b -> p (a b)")[:, 0:2 * 6 * P]
        modp = bank[0][:, 0:12 * BATCH].rearrange("p (m b) -> p m b", b=BATCH)
        mod = small[:, 32:32 + 12 * BATCH].rearrange("p (m b) -> p m b", b=BATCH)
        sgn = small[:, 128:128 + 4 * BATCH].rearrange("p (m b) -> p m b", b=BATCH)
        mag = small[:, 160:160 + 4 * BATCH].rearrange("p (m b) -> p m b", b=BATCH)
        s48 = small[0:48, 192:192 + NS]
        s24 = small[0:24, 208:208 + EXPERTS]

        with nc.Block() as block:
            @block.sync
            def _(sp):
                sp.dma_start(cm, cmod).then_inc(ld, 16)
                sp.dma_start(wm, wmod).then_inc(ld, 16)
                sp.dma_start(V[:], vecs).then_inc(ld, 16)
                sp.dma_start(wx.rearrange("p a j k -> p (a j k)"), pre).then_inc(ld, 16)
                sp.dma_start(W[:], wts).then_inc(ld, 16)
                sp.wait_ge(ld, 80)

            @block.gpsimd
            def _(pool):
                nc.gpsimd.memset(ident[:], 0.0).then_inc(pp, 1)
                nc.gpsimd.memset(ones[:], 1.0).then_inc(pp, 1)
                nc.gpsimd.memset(mhalf[:], -0.5).then_inc(pp, 1)
                nc.gpsimd.memset(starts[:], 0.0).then_inc(pp, 1)
                nc.gpsimd.iota(iota_e[:], pattern=[[1, EXPERTS]], base=0, channel_multiplier=0,
                               allow_small_or_imprecise_dtypes=True).then_inc(pp, 1)
                pool.wait_ge(pp, 5)
                nc.gpsimd.affine_select(out=ident[:], in_=ident[:], compare_op=ALU.not_equal, fill=1.0, base=0,
                                        pattern=[[-1, P]], channel_multiplier=1).then_inc(pp, 1)
                nc.gpsimd.memset(starts[:, 0:L:CHUNK], 1.0).then_inc(pp, 1)

            @block.scalar
            def _(act):
                act.wait_ge(ld, 80)
                nc.scalar.activation(cms, cm, ACT.Silu).then_inc(pa, 1)
                nc.scalar.activation(neg_a[:].rearrange("p a b -> p (a b)"), v("a_log", 0, ND * NS),
                                     ACT.Exp).then_inc(pa, 1)
                nc.scalar.activation(eig_half[:], v("eig"), ACT.Tanh).then_inc(pa, 1)

            @block.tensor
            def _(pe):
                pe.wait_ge(pa, 1)
                for m in range(12):
                    last = nc.tensor.matmul(modp[:, m, :], wm[:, m * P:(m + 1) * P],
                                            cms[:, (m // 6) * BATCH:(m // 6 + 1) * BATCH], start=True, stop=True)
                last.then_inc(pt, 1)
                for k in range(ND):
                    for j in range(ND):
                        last = nc.tensor.matmul(bank[1][:, k * DI:(k + 1) * DI], wx[:, 0, j, k * P:(k + 1) * P],
                                                wx[:, 1, j, :], start=(j == 0), stop=(j == ND - 1))
                last.then_inc(pt, 1)

            @block.vector
            def _(dve):
                steps = [0]

                def link(ins):
                    steps[0] += 1
                    ins.then_inc(pv, 1)
                    dve.wait_ge(pv, steps[0])

                dve.wait_ge(pp, 7)
                link(nc.vector.tensor_tensor(s48, ident[0:48, 0:16], ident[0:48, 16:32], ALU.add))
                link(nc.vector.tensor_tensor(s48, s48, ident[0:48, 32:48], ALU.add))
                link(nc.vector.tensor_copy(sel_b[:], s48[:, :, None].to_broadcast([48, NS, P])))
                link(nc.vector.tensor_tensor(s24, ident[0:24, 0:8], ident[0:24, 8:16], ALU.add))
                link(nc.vector.tensor_tensor(s24, s24, ident[0:24, 16:24], ALU.add))
                link(nc.vector.tensor_copy(sel_g[:], s24[:, :, None].to_broadcast([24, EXPERTS, RANK])))
                dve.wait_ge(pa, 3)
                link(nc.vector.tensor_scalar(neg_a[:], neg_a[:], -1.0, None, ALU.mult))
                link(nc.vector.tensor_scalar(eig_half[:], eig_half[:], 0.5, None, ALU.mult))
                link(nc.vector.tensor_scalar(gate_bh[:], v("gate_b", 0, 2), 0.5, None, ALU.mult))
                dve.wait_ge(pt, 2)
                link(nc.vector.tensor_copy(w_dtx[:].rearrange("p a b -> p (a b)"), bank[1][:]))
                link(nc.vector.tensor_copy(mod, modp))
                gates = mod[:, 2:12:3, :]
                link(nc.vector.tensor_scalar(sgn, gates, 0.0, 2.0, ALU.is_ge, ALU.mult))
                link(nc.vector.tensor_scalar(mag, gates, -1.0, None, ALU.mult))
                link(nc.vector.tensor_tensor(mag, mag, gates, ALU.max))
                link(nc.vector.tensor_scalar(mag, mag, 0.25, None, ALU.max))
                link(nc.vector.scalar_tensor_tensor(out=mag, in0=sgn, scalar=-1.0, in1=mag, op0=ALU.add,
                                                    op1=ALU.mult))
                for i, m in ((SA0, 0), (SB0, 3), (SA1, 6), (SB1, 9)):
                    link(nc.vector.tensor_copy(vec[:, :, i], mod[:, m, :]))
                for i, m in ((CA0, 1), (CB0, 4), (CA1, 7), (CB1, 10)):
                    link(nc.vector.tensor_scalar(vec[:, :, i], mod[:, m, :], 1.0, None, ALU.add))
                for i, g, col in ((G_LN, 0, v("ln_g")), (G_LB, 0, v("ln_b")), (G_FFN, 1, v("w3_s"))):
                    link(nc.vector.tensor_scalar(vec[:, :, i], mag[:, g, :], col, None, ALU.mult))
                link(nc.vector.tensor_scalar(vec[:, :, G_ATT], mag[:, 2, :], 0.5, None, ALU.mult))
                link(nc.vector.tensor_scalar(vec[:, :, G_MOE], mag[:, 3, :], 2.0, None, ALU.mult))

        def body(do_scan, do_rest, b):
            plan = rest_plan(do_scan)
            banks = bank_plan(do_scan, do_rest, plan)

            def full(eng, name):
                k, n, _, _ = banks[name]
                eng.wait_ge(bank_full[k], n + 1)
                return bank[k]

            def take(pe, name):
                k, _, reader, count = banks[name]
                if reader:
                    pe.wait_ge(s[reader], count)
                return bank[k]

            def filled(ins, name):
                ins.then_inc(bank_full[banks[name][0]], 1)

            with nc.Block() as block:
                @block.sync
                def _(sp):
                    if do_scan:
                        sp.dma_start(xt, x[bass.ds(b, 1)].rearrange("o (j p) c -> p (o j) c", p=P)).then_inc(s["x_in"], 16)
                    if do_rest:
                        sp.dma_start(xr[:], x[bass.ds(b - 1, 1)].rearrange("o (j p) c -> p (o j) c", p=P)).then_inc(
                            s["rest_x_in"], 16)
                        sp.wait_ge(s["x_upd"], 7)
                        sp.dma_start(out[bass.ds(b - 1, 1)].rearrange("o (j p) c -> p (o j) c", p=P), xr[:]).then_inc(
                            s["stored"], 16)
                        sp.wait_ge(s["stored"], 16)

                @block.tensor
                def _(pe):
                    def turn(name, src, sem, count):
                        pe.wait_ge(sem, count)
                        o = take(pe, name)
                        for jj in range(TH):
                            last = nc.tensor.transpose(o[:, jj * P:(jj + 1) * P], src(jj), ident[:])
                        filled(last, name)

                    def mixer_out():
                        pe.wait_ge(s["diag"], 5)
                        for name, a, n in (("rows0", 0, 4), ("rows1", 4, 1)):
                            o = take(pe, name)
                            for i in range(n):
                                last = nc.tensor.matmul(o[:, i * P:(i + 1) * P], ones[:], diag[:, a + i, :],
                                                        start=True, stop=True)
                            filled(last, name)
                        for h in range(2):
                            o = take(pe, ("mix", h))
                            for jj in range(TH):
                                t = (h * TH + jj) * P
                                for k in range(ND + 1):
                                    rhs = w("w_out", P, k * P) if k < ND else ident[:]
                                    last = nc.tensor.matmul(o[:, jj * P:(jj + 1) * P], ycm[:, k, t:t + P], rhs,
                                                            start=(k == 0), stop=(k == ND))
                            filled(last, ("mix", h))

                    def mixer_in():
                        for h in range(2):
                            turn(("in_t", h), lambda jj: xn[:, h * TH + jj, :], s["p_norm"], 4 * (h + 1))
                        for part, at in (("xs", 0), ("z", DI)):
                            for d in range(ND):
                                for h in range(2):
                                    pe.wait_ge(s["hcm"], h + 1)
                                    o = take(pe, (part, d, h))
                                    filled(nc.tensor.matmul(o[:], w("w_in", P, at + d * P), half(ycm[:, ND, :], h),
                                                            start=True, stop=True), (part, d, h))
                        pe.wait_ge(s["u"], 2)
                        for m in range(ND):
                            for h in range(2):
                                o = take(pe, ("dt", m, h))
                                for k in range(ND):
                                    last = nc.tensor.matmul(o[:], w_dtx[:, k, m * P:(m + 1) * P], half(u[:, k, :], h),
                                                            start=(k == 0), stop=(k == ND - 1))
                                filled(last, ("dt", m, h))
                        o = take(pe, "bc")
                        for j in range(NT):
                            for k in range(ND):
                                last = nc.tensor.matmul(o[:, j * 2 * NS:(j + 1) * 2 * NS], u[:, k, j * P:(j + 1) * P],
                                                        w("w_bc", 2 * NS, k * 2 * NS), start=(k == 0),
                                                        stop=(k == ND - 1))
                        filled(last, "bc")
                        pe.wait_ge(s["bc_split"], 5)
                        for h in range(2):
                            o = take(pe, ("b_t", h))
                            for jj in range(TH):
                                last = nc.tensor.transpose(o[0:SPLIT * NS, jj * P:(jj + 1) * P],
                                                           b_tok[:, h * TH + jj, :], ident[:])
                            filled(last, ("b_t", h))

                    def scan(t):
                        n, c = t // 2, t % 2
                        if n + 3 < NS:
                            i = 2 * (n + 3) + c
                            if i == 0:
                                pe.wait_ge(s["b_sb"], 2)
                            else:
                                pe.wait_ge(s["b_spread"], i)
                            nc.tensor.matmul(bspr[:], sel_b[:, n + 3, :], half(b_sb[:], c), start=True,
                                             stop=True).then_inc(s["b_full"], 1)
                        if t >= 0:
                            pe.wait_ge(s["h_done"], 2 * n + 2)
                            if n >= 1:
                                pe.wait_ge(s["acc"], TH * (2 * n - 1 + c))
                            for jj in range(TH):
                                for d in range(ND):
                                    at = (c * TH + jj) * P
                                    last = nc.tensor.transpose(ht[c][:, jj, d * P:(d + 1) * P],
                                                               hst[:, (2 * n + d) % 4, at:at + P], ident[:])
                            last.then_inc(s["ht_full"], 1)

                    def rest(stage):
                        kind = stage[0]
                        if kind == "norm":
                            n = stage[1]
                            for h in range(2):
                                turn(("norm_t", n, h), lambda jj: rn[:, h * TH + jj, :], s["r_norm"], 8 * n + 4 * (h + 1))
                        elif kind == "gated":
                            h, m = stage[1:]
                            pe.wait_ge(s["hc"], 2)
                            for part, wt in (("gated_a", "w1"), ("gated_b", "w2")):
                                o = take(pe, (part, h, m))
                                filled(nc.tensor.matmul(o[:], w(wt, P, m * P), half(hc[:], h), start=True, stop=True),
                                       (part, h, m))
                        elif kind in ("hidden1", "hidden2"):
                            h, m = stage[1:]
                            wt, src, sem = ("h1", h0, s["h0"]) if kind == "hidden1" else ("h2", g1, s["g1"])
                            o = take(pe, stage)
                            for k in range(NM):
                                if m == 0:
                                    pe.wait_ge(sem, NM * h + k + 1)
                                last = nc.tensor.matmul(o[:], w(wt, P, k * HID + m * P), src[:, k, :], start=(k == 0),
                                                        stop=(k == NM - 1))
                            filled(last, stage)
                        elif kind == "down":
                            h = stage[1]
                            pe.wait_ge(s["g2"], NM * (h + 1))
                            pe.wait_ge(s["w3g"], 1)
                            o = take(pe, stage)
                            for jj in range(TH):
                                for k in range(NM):
                                    last = nc.tensor.matmul(o[:, jj * P:(jj + 1) * P], g2[:, k, jj * P:(jj + 1) * P],
                                                            w3g[:, k, :], start=(k == 0), stop=(k == NM - 1))
                            filled(last, stage)
                        elif kind == "proj":
                            pe.wait_ge(s["hc"], 4)
                            for h in range(2):
                                o = take(pe, ("proj", h))
                                for jj in range(TH):
                                    t = (h * TH + jj) * P
                                    last = nc.tensor.matmul(o[:, jj * P:(jj + 1) * P], hc[:, t:t + P], w("b_in", P),
                                                            start=True, stop=True)
                                filled(last, ("proj", h))
                            for h in range(2):
                                turn(("norm_t", 3, h), lambda jj: rn[:, h * TH + jj, :], s["r_norm"], 8 * 3 + 4 * (h + 1))
                        elif kind == "gates":
                            pe.wait_ge(s["xpc"], 2)
                            for h in range(2):
                                for i, part in enumerate(("alpha", "beta")):
                                    o = take(pe, (part, h))
                                    filled(nc.tensor.matmul(o[:], w("b_gate", P, i * P), half(xpc, h), start=True,
                                                            stop=True), (part, h))
                        elif kind == "att_out":
                            pe.wait_ge(s["hout"], 1)
                            pe.wait_ge(s["wog"], 1)
                            for h in range(2):
                                o = take(pe, ("att_out", h))
                                for jj in range(TH):
                                    t = (h * TH + jj) * P
                                    last = nc.tensor.matmul(o[:, jj * P:(jj + 1) * P], rec[:, t:t + P], wog[:],
                                                            start=True, stop=True)
                                filled(last, ("att_out", h))
                        elif kind == "route":
                            pe.wait_ge(s["hc"], 6)
                            o = take(pe, "logits")
                            for j in range(NT):
                                last = nc.tensor.matmul(o[:, j * EXPERTS:(j + 1) * EXPERTS], hc[:, j * P:(j + 1) * P],
                                                        w("e_gate", EXPERTS), start=True, stop=True)
                            filled(last, "logits")
                            pe.wait_ge(s["g_split"], 5)
                            for h in range(2):
                                o = take(pe, ("g_t", h))
                                for jj in range(TH):
                                    last = nc.tensor.transpose(o[0:SPLIT * EXPERTS, jj * P:(jj + 1) * P],
                                                               g_tok[:, h * TH + jj, :], ident[:])
                                filled(last, ("g_t", h))
                        elif kind == "expert":
                            h, m = stage[1:]
                            pe.wait_ge(s["gs"], 2)
                            o = take(pe, ("exp_h", h, m))
                            filled(nc.tensor.matmul(o[:], w("e1", P, m * P), half(hc[:], h), start=True, stop=True),
                                   ("exp_h", h, m))
                            o = take(pe, ("exp_g", h, m))
                            filled(nc.tensor.matmul(o[:], sel_g[:, 2 * m:2 * m + 2, :].rearrange("p a b -> p (a b)"),
                                                    half(g_sb[:], h), start=True, stop=True), ("exp_g", h, m))
                        elif kind == "combine":
                            h = stage[1]
                            pe.wait_ge(s["gx"], NM * (h + 1))
                            pe.wait_ge(s["w2g"], 1)
                            o = take(pe, stage)
                            for jj in range(TH):
                                for k in range(NM):
                                    last = nc.tensor.matmul(o[:, jj * P:(jj + 1) * P], h0[:, k, jj * P:(jj + 1) * P],
                                                            w2g[:, k, :], start=(k == 0), stop=(k == NM - 1))
                            filled(last, stage)

                    if do_rest:
                        mixer_out()
                    if do_scan:
                        mixer_in()
                    for t in TICKS:
                        if do_scan:
                            scan(t)
                        if do_rest:
                            for stage in plan[t]:
                                rest(stage)
                    if do_scan:
                        pe.wait_ge(s["acc"], NT * NS)
                        for d in range(ND):
                            for h in range(2):
                                o = take(pe, ("y_t", d, h))
                                for jj in range(TH):
                                    last = nc.tensor.transpose(o[:, jj * P:(jj + 1) * P],
                                                               acc[:, h * TH + jj, d * P:(d + 1) * P], ident[:])
                                filled(last, ("y_t", d, h))

                @block.scalar
                def _(act):
                    def mixer_in():
                        for h in range(2):
                            o = full(act, ("in_t", h))
                            act.wait_ge(s["cur"], 1)
                            if do_rest and h == 0:
                                full(act, ("mix", 1))
                            nc.scalar.activation(half(ycm[:, ND, :], h), o[:], ACT.Identity,
                                                       bias=cur[:, SA0:SA0 + 1], scale=cur[:, CA0:CA0 + 1]).then_inc(s["hcm"], 1)
                        for d in range(ND):
                            for h in range(2):
                                o = full(act, ("xs", d, h))
                                at = TAPS - 1 + h * HALF
                                nc.scalar.activation(xpad[:, d, at:at + HALF], o[:], ACT.Copy).then_inc(s["xs_sb"], 1)
                        for d in range(ND):
                            for h in range(2):
                                o = full(act, ("z", d, h))
                                nc.scalar.activation(half(zs[:, d, :], h), o[:], ACT.Silu).then_inc(s["z"], 1)
                        for d in range(ND):
                            act.wait_ge(s["conv"], TAPS * (d + 1))
                            nc.scalar.activation(u[:, d, :], u[:, d, :], ACT.Silu,
                                                 bias=v("conv_b", d)).then_inc(s["u"], 1)
                        for d in range(ND):
                            for h in range(2):
                                o = full(act, ("dt", d, h))
                                nc.scalar.activation(half(delta[:, d, :], h), o[:], ACT.Relu,
                                                     bias=v("b_dt", d)).then_inc(s["relu_dt"], 1)
                                nc.scalar.activation(half(soft[:, d, :], h), o[:], ACT.Abs, bias=v("b_dt", d)).then_inc(s["abs_dt"], 1)
                        act.wait_ge(s["abs_dt"], 4)
                        nc.scalar.activation(soft, soft, ACT.Exp, scale=-1.0).then_inc(s["exp_dt"], 1)
                        act.wait_ge(s["exp_dt"], 1)
                        nc.scalar.activation(soft, soft, ACT.Ln, bias=1.0).then_inc(s["ln_dt"], 1)
                        for h in range(2):
                            o = full(act, ("b_t", h))
                            nc.scalar.activation(half(b_sb[:], h), o[0:SPLIT * NS, :], ACT.Copy).then_inc(s["b_sb"], 1)

                    def scan(t):
                        n, c = t // 2, t % 2
                        if n + 3 < NS:
                            m = n + 3
                            act.wait_ge(s["b_full"], 2 * m + c + 1)
                            if m >= 2:
                                act.wait_ge(s["dbu"], 2 * m - 2)
                            nc.scalar.activation(half(b_spread[:, m % 2, :], c), bspr[:], ACT.Copy).then_inc(
                                s["b_spread"], 1)
                        if 0 <= n + 2 < NS:
                            i = 2 * (n + 2) + c
                            act.wait_ge(s["delta"], 2)
                            if i >= 4:
                                act.wait_ge(s["h_done"], i - 3)
                            nc.scalar.activation(da[:, i % 4, :], delta[:, c, :], ACT.Exp,
                                                 scale=neg_a[:, c, n + 2:n + 3]).then_inc(s["da"], 1)

                    def turned(n, bias, scale):
                        for h in range(2):
                            o = full(act, ("norm_t", n, h))
                            nc.scalar.activation(half(hc[:], h), o[:], ACT.Identity, bias=cur_r[:, bias:bias + 1],
                                                       scale=cur_r[:, scale:scale + 1]).then_inc(s["hc"], 1)

                    def rest(stage):
                        kind = stage[0]
                        if kind == "norm":
                            bias, scale = {1: (SB0, CB0), 2: (SA1, CA1), 4: (SB1, CB1)}[stage[1]]
                            turned(stage[1], bias, scale)
                        elif kind == "gated":
                            h, m = stage[1:]
                            o = full(act, ("gated_a", h, m))
                            if NM * h + m:
                                act.wait_ge(s["h0"], NM * h + m)
                            nc.scalar.activation(ga[:], o[:], ACT.Silu, scale=v("w1_s", m)).then_inc(s["gate_a"], 1)
                        elif kind in ("hidden1", "hidden2"):
                            h, m = stage[1:]
                            dst, col, sem = (g1, "h1_s", s["g1"]) if kind == "hidden1" else (g2, "h2_s", s["g2"])
                            o = full(act, stage)
                            nc.scalar.activation(dst[:, m, :], o[:], ACT.Gelu, scale=v(col, m)).then_inc(sem, 1)
                        elif kind == "proj":
                            for h in range(2):
                                o = full(act, ("norm_t", 3, h))
                                nc.scalar.activation(half(xpc, h), o[:], ACT.Identity, bias=v("l_b"),
                                                           scale=v("l_g")).then_inc(s["xpc"], 1)
                        elif kind == "gates":
                            for h in range(2):
                                for i, (part, dst, sem) in enumerate((("alpha", al, s["tanh_a"]), ("beta", bb, s["tanh_b"]))):
                                    o = full(act, (part, h))
                                    nc.scalar.activation(half(dst, h), o[:], ACT.Tanh, bias=gate_bh[:, i:i + 1],
                                                               scale=0.5).then_inc(sem, 1)
                        elif kind == "recur":
                            act.wait_ge(s["cp"], 1)
                            nc.scalar.activation(rec[:], rec[:], ACT.Abs).then_inc(s["cp_abs"], 1)
                        elif kind == "route":
                            act.wait_ge(s["gap"], 1)
                            nc.scalar.activation(gap[:, :, 0:1], gap[:, :, 0:1], ACT.Tanh, scale=0.5).then_inc(s["tg"], 1)
                            for h in range(2):
                                o = full(act, ("g_t", h))
                                nc.scalar.activation(half(g_sb[:], h), o[0:SPLIT * EXPERTS, :], ACT.Copy).then_inc(s["gs"], 1)
                        elif kind == "expert":
                            h, m = stage[1:]
                            o = full(act, ("exp_h", h, m))
                            if h == 1 and m == 0:
                                act.wait_ge(s["x_upd"], 6)
                            nc.scalar.activation(h0[:, m, :], o[:], ACT.Gelu).then_inc(s["exp_g"], 1)

                    if do_scan:
                        mixer_in()
                    for t in TICKS:
                        if do_scan:
                            scan(t)
                        if do_rest:
                            for stage in plan[t]:
                                rest(stage)

                @block.gpsimd
                def _(pool):
                    def inv_std(n, h, ag, vr, rs, s_ag, s_vr, s_rs):
                        j = slice(h * TH, (h + 1) * TH)
                        pool.wait_ge(s_ag, 8 * n + 4 * (h + 1))
                        nc.gpsimd.tensor_scalar(vr[:, j], ag[:, j, 1], EPS, None, ALU.add).then_inc(s_vr, 1)
                        pool.wait_ge(s_vr, 2 * n + h + 1)
                        nc.gpsimd.tensor_tensor(rs[:, j], vr[:, j], mhalf[:, j], ALU.pow).then_inc(s_rs, 1)

                    def rest_norm(n):
                        for h in range(2):
                            inv_std(n, h, raggr, rvar, rrstd, s["r_aggr"], s["r_var"], s["r_rstd"])

                    def scan(t):
                        n, c = t // 2, t % 2
                        if 0 <= n + 2 < NS:
                            i = 2 * (n + 2) + c
                            pool.wait_ge(s["b_spread"], 2 * (n + 2) + 2)
                            if i >= 4:
                                pool.wait_ge(s["h_done"], i - 3)
                            nc.gpsimd.tensor_tensor(dbu[:, i % 4, :], du[:, c, :], b_spread[:, (n + 2) % 2, :],
                                                    ALU.mult).then_inc(s["dbu"], 1)

                    def rest(stage):
                        kind = stage[0]
                        if kind == "norm":
                            rest_norm(stage[1])
                        elif kind == "proj":
                            rest_norm(3)

                    if do_rest:
                        rest_norm(0)
                    if do_scan:
                        for h in range(2):
                            inv_std(0, h, aggr, var, rstd, s["p_aggr"], s["p_var"], s["p_rstd"])
                        for d in range(ND):
                            pool.wait_ge(s["delta"], d + 1)
                            nc.gpsimd.tensor_tensor(du[:, d, :], delta[:, d, :], u[:, d, :], ALU.mult).then_inc(s["du"], 1)
                        pool.wait_ge(s["du"], 2)
                    for t in TICKS:
                        if do_scan:
                            scan(t)
                        if do_rest:
                            for stage in plan[t]:
                                rest(stage)

                @block.vector
                def _(dve):
                    def norm(n, h, src, st, ag, rs, dst, s_st, s_ag, s_rs, s_nm):
                        for jj in range(TH):
                            nc.vector.bn_stats(st[:, h * TH + jj, :], src(jj)).then_inc(s_st, 1)
                        dve.wait_ge(s_st, 8 * n + 4 * (h + 1))
                        for jj in range(TH):
                            nc.vector.bn_aggr(ag[:, h * TH + jj, :], st[:, h * TH + jj, :]).then_inc(s_ag, 1)
                        dve.wait_ge(s_rs, 2 * n + h + 1)
                        for jj in range(TH):
                            j = h * TH + jj
                            last = nc.vector.tensor_scalar(dst[:, j, :], src(jj), ag[:, j, 0:1], rs[:, j:j + 1],
                                                           ALU.subtract, ALU.mult)
                            last.then_inc(s_nm, 1)

                    def rest_norm(n, h, src):
                        norm(n, h, src, rstat, raggr, rrstd, rn, s["r_stat"], s["r_aggr"], s["r_rstd"], s["r_norm"])

                    def add_half(name, h, count):
                        o = full(dve, name)
                        dve.wait_ge(s["x_upd"], count)
                        xh = xr[:, h * TH:(h + 1) * TH, :].rearrange("p j c -> p (j c)")
                        nc.vector.tensor_tensor(xh, o[:], xh, ALU.add).then_inc(s["x_upd"], 1)

                    def mixer_out():
                        nc.vector.tensor_copy(cur_r[:], vec[:, bass.ds(b - 1, 1), :].rearrange("p o n -> p (o n)")
                                              ).then_inc(s["cur_r"], 1)
                        dve.wait_ge(s["cur_r"], 1)
                        for i, col in enumerate((G_LN, G_LB, G_FFN, G_ATT, G_MOE)):
                            nc.vector.tensor_scalar(diag[:, i, :], ident[:], cur_r[:, col:col + 1], None,
                                                    ALU.mult).then_inc(s["diag"], 1)
                        o = full(dve, "rows0")
                        nc.vector.tensor_copy(rows[:].rearrange("p a c -> p (a c)"), o[:, 0:2 * P]).then_inc(s["rows"], 1)
                        nc.vector.tensor_tensor(w3g[:], w("w3", NM * P).rearrange("p (k c) -> p k c", k=NM),
                                                o[:, None, 2 * P:3 * P].to_broadcast([P, NM, P]), ALU.mult
                                                ).then_inc(s["w3g"], 1)
                        nc.vector.tensor_tensor(wog[:], w("b_out", P), o[:, 3 * P:4 * P], ALU.mult).then_inc(s["wog"], 1)
                        o = full(dve, "rows1")
                        nc.vector.tensor_tensor(w2g[:], w("e2", NM * P).rearrange("p (k c) -> p k c", k=NM),
                                                      o[:, None, 0:P].to_broadcast([P, NM, P]), ALU.mult).then_inc(s["w2g"], 1)
                        for h in range(2):
                            o = full(dve, ("mix", h))
                            rest_norm(0, h, lambda jj: o[:, jj * P:(jj + 1) * P])
                        dve.wait_ge(s["rest_x_in"], 16)
                        dve.wait_ge(s["rows"], 1)
                        nc.vector.tensor_tensor(xr[:], xr[:], rows[:, None, 1, :].to_broadcast([P, NT, P]),
                                                ALU.add).then_inc(s["x_g2"], 1)
                        dve.wait_ge(s["r_norm"], 8)
                        nc.vector.tensor_tensor(rn[:], rn[:], rows[:, None, 0, :].to_broadcast([P, NT, P]),
                                                ALU.mult).then_inc(s["on_g"], 1)
                        dve.wait_ge(s["on_g"], 1)
                        dve.wait_ge(s["x_g2"], 1)
                        nc.vector.tensor_tensor(xr[:], xr[:], rn[:], ALU.add).then_inc(s["x_upd"], 1)
                        dve.wait_ge(s["x_upd"], 1)

                    def split(dst, hi, n, parts, sem):
                        for i in range(parts - 1):
                            a, c = dst[:, :, i * n:(i + 1) * n], dst[:, :, (i + 1) * n:(i + 2) * n]
                            dve.wait_ge(sem, 2 * i + 1)
                            nc.vector.tensor_copy(hi[:, i, :, :], a).then_inc(sem, 1)
                            dve.wait_ge(sem, 2 * i + 2)
                            nc.vector.tensor_tensor(c, a, hi[:, i, :, :], ALU.subtract).then_inc(sem, 1)

                    def mixer_in():
                        nc.vector.tensor_copy(cur[:], vec[:, bass.ds(b, 1), :].rearrange("p o n -> p (o n)")
                                              ).then_inc(s["cur"], 1)
                        nc.vector.memset(xpad[:, :, 0:TAPS - 1], 0.0).then_inc(s["pad"], 1)
                        dve.wait_ge(s["x_in"], 16)
                        for h in range(2):
                            norm(0, h, lambda jj: xt[:, h * TH + jj, :], stat, aggr, rstd, xn, s["p_stat"], s["p_aggr"],
                                 s["p_rstd"], s["p_norm"])
                        dve.wait_ge(s["pad"], 1)
                        for d in range(ND):
                            dve.wait_ge(s["xs_sb"], 2 * (d + 1))
                            for k in range(TAPS):
                                tap = v("conv_w", d * TAPS + k)
                                if k == 0:
                                    ins = nc.vector.tensor_scalar(u[:, d, :], xpad[:, d, 0:L], tap, None, ALU.mult)
                                else:
                                    dve.wait_ge(s["conv"], TAPS * d + k)
                                    ins = nc.vector.scalar_tensor_tensor(out=u[:, d, :], in0=xpad[:, d, k:k + L],
                                                                         scalar=tap, in1=u[:, d, :], op0=ALU.mult,
                                                                         op1=ALU.add)
                                ins.then_inc(s["conv"], 1)
                        o = full(dve, "bc")[:, 0:NT * 2 * NS].rearrange("p (j n) -> p j n", n=2 * NS)
                        nc.vector.tensor_copy(b_tok[:, :, 0:NS], o[:, :, 0:NS]).then_inc(s["bc_split"], 1)
                        nc.vector.tensor_copy(c_tok[:], o[:, :, NS:2 * NS]).then_inc(s["c_sb"], 1)
                        split(b_tok, b_hi, NS, SPLIT, s["bc_split"])
                        dve.wait_ge(s["ln_dt"], 1)
                        for d in range(ND):
                            nc.vector.tensor_tensor(delta[:, d, :], delta[:, d, :], soft[:, d, :],
                                                    ALU.add).then_inc(s["delta"], 1)

                    def scan(t):
                        n, c = t // 2, t % 2
                        if 0 <= n + 1 < NS:
                            i = 2 * (n + 1) + c
                            dve.wait_ge(s["da"], i + 1)
                            dve.wait_ge(s["dbu"], i + 1)
                            if n >= 1:
                                dve.wait_ge(s["ht_full"], 2 * n)
                            nc.vector.tensor_tensor_scan(hst[:, i % 4, :], da[:, i % 4, :], dbu[:, i % 4, :], 0.0,
                                                         ALU.mult, ALU.add).then_inc(s["h_done"], 1)
                        if t >= 0:
                            dve.wait_ge(s["ht_full"], t + 1)
                            if n == 0:
                                dve.wait_ge(s["c_sb"], 1)
                            else:
                                dve.wait_ge(s["acc"], TH * (2 * n - 1 + c))
                            for jj in range(TH):
                                j = c * TH + jj
                                if n == 0:
                                    ins = nc.vector.tensor_scalar(acc[:, j, :], ht[c][:, jj, :], c_tok[:, j, 0:1], None,
                                                                  ALU.mult)
                                else:
                                    ins = nc.vector.scalar_tensor_tensor(out=acc[:, j, :], in0=ht[c][:, jj, :],
                                                                         scalar=c_tok[:, j, n:n + 1], in1=acc[:, j, :],
                                                                         op0=ALU.mult, op1=ALU.add)
                                ins.then_inc(s["acc"], 1)

                    def rest(stage):
                        kind = stage[0]
                        if kind == "norm":
                            n = stage[1]
                            for h in range(2):
                                dve.wait_ge(s["x_upd"], {1: 1, 2: 2 + h, 4: 4 + h}[n])
                                if h == 0:
                                    dve.wait_ge(s["hc"], 2 * {1: 0, 2: 1, 4: 2}[n]) if n > 1 else None
                                rest_norm(n, h, lambda jj: xr[:, h * TH + jj, :])
                        elif kind == "gated":
                            h, m = stage[1:]
                            o = full(dve, ("gated_b", h, m))
                            dve.wait_ge(s["gate_a"], NM * h + m + 1)
                            nc.vector.scalar_tensor_tensor(out=h0[:, m, :], in0=o[:], scalar=v("w2_s", m), in1=ga[:],
                                                                 op0=ALU.mult, op1=ALU.mult).then_inc(s["h0"], 1)
                        elif kind == "down":
                            add_half(stage, stage[1], stage[1] + 1)
                        elif kind == "proj":
                            for h in range(2):
                                o = full(dve, ("proj", h))
                                rest_norm(3, h, lambda jj: o[:, jj * P:(jj + 1) * P])
                        elif kind == "gates":
                            dve.wait_ge(s["tanh_a"], 2)
                            nc.vector.tensor_scalar(al, al, eig_half[:], eig_half[:], ALU.mult,
                                                    ALU.add).then_inc(s["alpha"], 1)
                            dve.wait_ge(s["alpha"], 1)
                            nc.vector.tensor_copy(ash[:, 1:L], al[:, 0:L - 1]).then_inc(s["a_shift"], 1)
                            dve.wait_ge(s["a_shift"], 1)
                            nc.vector.memset(ash[:, 0:L:CHUNK], 0.0).then_inc(s["a_shift"], 1)
                            dve.wait_ge(s["tanh_b"], 2)
                            nc.vector.scalar_tensor_tensor(out=bb, in0=bb, scalar=1.0, in1=xpc, op0=ALU.add,
                                                           op1=ALU.mult).then_inc(s["b_in"], 1)
                        elif kind == "recur":
                            dve.wait_ge(s["a_shift"], 2)
                            nc.vector.tensor_tensor_scan(rec[:], ash, starts[:], 0.0, ALU.mult,
                                                         ALU.add).then_inc(s["cp"], 1)
                            dve.wait_ge(s["cp_abs"], 1)
                            dve.wait_ge(s["b_in"], 1)
                            nc.vector.scalar_tensor_tensor(out=rec[:], in0=rec[:], scalar=1e-8, in1=bb, op0=ALU.is_gt,
                                                           op1=ALU.mult).then_inc(s["bg_in"], 1)
                            dve.wait_ge(s["bg_in"], 1)
                            nc.vector.tensor_tensor(rec[:], rec[:], al, ALU.mult).then_inc(s["c_in"], 1)
                            dve.wait_ge(s["c_in"], 1)
                            nc.vector.tensor_copy(rec[:, CHUNK - 1:L:CHUNK], bb[:, CHUNK - 1:L:CHUNK]).then_inc(s["c_last"], 1)
                            nc.vector.memset(qs[:, 0:1], 0.0).then_inc(s["q0"], 1)
                            dve.wait_ge(s["c_last"], 1)
                            nc.vector.tensor_tensor_scan(qs[:, 1:L + 1], al, rec[:], 0.0, ALU.mult,
                                                         ALU.add).then_inc(s["q"], 1)
                            dve.wait_ge(s["q"], 1)
                            dve.wait_ge(s["q0"], 1)
                            nc.vector.tensor_tensor(rec[:], al, qs[:, 0:L], ALU.mult).then_inc(s["aq"], 1)
                            dve.wait_ge(s["aq"], 1)
                            nc.vector.tensor_tensor(rec[:], rec[:], bb, ALU.add).then_inc(s["hout"], 1)
                        elif kind == "att_out":
                            for h in range(2):
                                add_half(("att_out", h), h, 3 + h)
                        elif kind == "route":
                            o = full(dve, "logits")[:, 0:NT * EXPERTS].rearrange("p (j e) -> p j e", e=EXPERTS)
                            nc.vector.tensor_tensor(lg[:], o, v("bg", 0, EXPERTS)[:, None, :].to_broadcast(
                                [P, NT, EXPERTS]), ALU.add).then_inc(s["lg"], 1)
                            dve.wait_ge(s["lg"], 1)
                            for j in range(NT):
                                nc.vector.max(top[:, j, :], lg[:, j, :]).then_inc(s["top"], 1)
                            dve.wait_ge(s["top"], NT)
                            for j in range(NT):
                                nc.vector.max_index(idx[:, j, :], top[:, j, :], lg[:, j, :]).then_inc(s["idx"], 1)
                            nc.vector.tensor_tensor(gap[:, :, 0:1], top[:, :, 0:1], top[:, :, 1:2],
                                                    ALU.subtract).then_inc(s["gap"], 1)
                            dve.wait_ge(s["idx"], NT)
                            nc.vector.tensor_copy(idf[:], idx[:]).then_inc(s["one"], 1)
                            dve.wait_ge(s["one"], 1)
                            for i in range(2):
                                nc.vector.tensor_tensor(oh[:, i, :, :], iota_e[:, None, :].to_broadcast([P, NT, EXPERTS]),
                                                        idf[:, :, i:i + 1].to_broadcast([P, NT, EXPERTS]),
                                                        ALU.is_equal).then_inc(s["one"], 1)
                            dve.wait_ge(s["tg"], 1)
                            nc.vector.tensor_scalar(gap[:, :, 1:2], gap[:, :, 0:1], -0.5, 0.5, ALU.mult,
                                                    ALU.add).then_inc(s["wts"], 1)
                            dve.wait_ge(s["wts"], 1)
                            nc.vector.tensor_scalar(gap[:, :, 0:1], gap[:, :, 0:1], 0.5, 0.5, ALU.mult,
                                                    ALU.add).then_inc(s["wts"], 1)
                            dve.wait_ge(s["wts"], 2)
                            dve.wait_ge(s["one"], 3)
                            for i in range(2):
                                nc.vector.tensor_tensor(oh[:, i, :, :], oh[:, i, :, :],
                                                        gap[:, :, i:i + 1].to_broadcast([P, NT, EXPERTS]),
                                                        ALU.mult).then_inc(s["one"], 1)
                            dve.wait_ge(s["one"], 5)
                            nc.vector.tensor_tensor(g_tok[:, :, 0:EXPERTS], oh[:, 0, :, :], oh[:, 1, :, :],
                                                    ALU.add).then_inc(s["g_split"], 1)
                            split(g_tok, g_hi, EXPERTS, SPLIT, s["g_split"])
                        elif kind == "expert":
                            h, m = stage[1:]
                            o = full(dve, ("exp_g", h, m))
                            dve.wait_ge(s["exp_g"], NM * h + m + 1)
                            nc.vector.tensor_tensor(h0[:, m, :], o[:], h0[:, m, :], ALU.mult).then_inc(s["gx"], 1)
                        elif kind == "combine":
                            add_half(stage, stage[1], stage[1] + 5)

                    if do_rest:
                        mixer_out()
                    if do_scan:
                        mixer_in()
                    for t in TICKS:
                        if do_scan:
                            scan(t)
                        if do_rest:
                            for stage in plan[t]:
                                rest(stage)
                    if do_scan:
                        dve.wait_ge(s["z"], 4)
                        for d in range(ND):
                            for h in range(2):
                                o = full(dve, ("y_t", d, h))
                                i = 2 * d + h + 1
                                nc.vector.scalar_tensor_tensor(out=half(ycm[:, d, :], h), in0=half(u[:, d, :], h),
                                                                     scalar=v("d", d), in1=o[:], op0=ALU.mult,
                                                                     op1=ALU.add).then_inc(s["y_sum"], 1)
                                dve.wait_ge(s["y_sum"], i)
                                nc.vector.tensor_tensor(half(ycm[:, d, :], h), half(ycm[:, d, :], h),
                                                        half(zs[:, d, :], h), ALU.mult).then_inc(s["y"], 1)

            for q in clear:
                nc.gpsimd.sem_clear(q)
            nc.all_engine_barrier(sem_only=True)

        body(True, False, 0)
        with nc.Fori(1, BATCH) as b:
            body(True, True, b)
        body(False, True, BATCH)


def kernel(**inputs):
    import numpy as np
    import concourse.bacc as bacc
    from concourse.bass_utils import run_bass_kernel_spmd

    a = {k: np.asarray(t) for k, t in inputs.items()}

    def rows_to(t):
        n = t.shape[0] // P
        return np.ascontiguousarray(t.reshape(n, P, -1).transpose(1, 0, 2).reshape(P, -1))

    wx = a["L0_attn_W_x"]
    gate = a["L1_attn_W_gate"]
    spread = lambda t: np.repeat(t, P // HEADS, axis=0)
    wts = np.concatenate([
        a["L0_attn_W_in"].T, rows_to(wx[DI:].T), rows_to(a["L0_attn_W_out"].T), a["L0_ffn_w1_w"].T,
        a["L0_ffn_w2_w"].T, rows_to(a["L0_ffn_h1_w"].T), rows_to(a["L0_ffn_h2_w"].T), rows_to(a["L0_ffn_w3_w"].T),
        a["L1_attn_W_in"].T, spread(gate[:HEADS]).T, spread(gate[HEADS:]).T, a["L1_attn_W_out"].T,
        a["L1_ffn_W1"].reshape(EXPERTS * RANK, P).T, rows_to(a["L1_ffn_W2"].transpose(0, 2, 1).reshape(-1, P)),
        a["L1_ffn_Wg"].T], axis=1)
    col = lambda t: rows_to(t.reshape(-1, 1))
    vecs = np.concatenate([
        rows_to(a["L0_attn_conv_w"].reshape(DI, TAPS)), col(a["L0_attn_conv_b"]), col(a["L0_attn_b_dt"]),
        rows_to(a["L0_attn_A_log"]), col(a["L0_attn_D"]), col(a["L0_attn_ln_g"]), col(a["L0_attn_ln_b"]),
        col(a["L0_ffn_w1_s"]), col(a["L0_ffn_w2_s"]), col(a["L0_ffn_h1_s"]), col(a["L0_ffn_h2_s"]),
        col(a["L0_ffn_w3_s"]), col(a["L1_attn_ln_g"]), col(a["L1_attn_ln_b"]),
        col(spread(a["L1_attn_b_gate"][:HEADS])), col(spread(a["L1_attn_b_gate"][HEADS:])),
        col(spread(a["L1_attn_eig_raw"])), np.broadcast_to(a["L1_ffn_bg"], (P, EXPERTS))], axis=1)
    pre = np.concatenate([rows_to(wx[:DI]), rows_to(a["L0_attn_W_dt"].T)], axis=1)
    cmod = np.concatenate([a["L0_c"].T, a["L1_c"].T], axis=1)
    wmod = np.concatenate([a["L0_wmod"], a["L1_wmod"]], axis=1)
    arrays = {"in_x": a["L0_attn_x"], "in_wts": wts, "in_vecs": vecs, "in_pre": pre, "in_cmod": cmod, "in_wmod": wmod}
    arrays = {k: np.ascontiguousarray(t) for k, t in arrays.items()}

    nc = bacc.Bacc("TRN2", target_bir_lowering=False, num_devices=1)
    args = [nc.dram_tensor(k, t.shape, mybir.dt.from_np(t.dtype), kind="ExternalInput").ap() for k, t in arrays.items()]
    args.append(nc.dram_tensor("out_0", (BATCH, L, P), F32, kind="ExternalOutput").ap())
    build(nc, *args)
    r = run_bass_kernel_spmd(nc, [arrays], core_ids=[0])
    return r.results[0]["out_0"]
```

```python
from contextlib import ExitStack

import concourse.bass as bass
from concourse import mybir

F32 = mybir.dt.float32
BF16 = mybir.dt.bfloat16
U32 = mybir.dt.uint32
ALU = mybir.AluOpType
ACT = mybir.ActivationFunctionType

P = 128
BATCH, L = 8, 1024
NT = L // P
HALF = 512
TH = HALF // P
DI = 256
ND = DI // P
NS = 16
TAPS = 4
HID = 512
NM = HID // P
EXPERTS, RANK = 8, 64
CHUNK = 16
HEADS = 16
EPS = 1e-5
SPLIT = 3

W_PARTS = [("w_in", 2 * DI), ("w_bc", ND * 2 * NS), ("w_out", ND * P), ("w1", HID), ("w2", HID), ("h1", NM * HID),
           ("h2", NM * HID), ("w3", NM * P), ("b_in", P), ("b_gate", 2 * P), ("b_out", P), ("e1", HID),
           ("e2", NM * P), ("e_gate", EXPERTS)]
W_AT, W_COLS = {}, 0
for _name, _n in W_PARTS:
    W_AT[_name] = W_COLS
    W_COLS += _n
V_PARTS = [("conv_w", ND * TAPS), ("conv_b", ND), ("b_dt", ND), ("a_log", ND * NS), ("d", ND), ("ln_g", 1),
           ("ln_b", 1), ("w1_s", NM), ("w2_s", NM), ("h1_s", NM), ("h2_s", NM), ("w3_s", 1), ("l_g", 1), ("l_b", 1),
           ("gate_b", 2), ("eig", 1), ("bg", EXPERTS)]
V_AT, V_COLS = {}, 0
for _name, _n in V_PARTS:
    V_AT[_name] = V_COLS
    V_COLS += _n
(SA0, CA0, G_LN, G_LB, SB0, CB0, G_FFN, SA1, CA1, G_ATT, SB1, CB1, G_MOE) = range(13)
NVEC = 13


RING = 6
EXPS = 4
STEPS_IN = 8
TICKS = range(-6, 2 * NS + 1)
SLOTS = [("in", k) for k in range(STEPS_IN)] + [("scan", t) for t in TICKS] + [("out", 0)]
IN_ROOM = 4.5
SCAN_ROOM = 2.45


def rest_stages():
    out = [(("rows",), 1, 0)]
    out += [(("mix", h), 2.6, 0) for h in range(2)]
    out += [((kind, 0, h), 0, 0) for h in range(2) for kind in ("stat", "rstd")]
    out += [(("apply", 0, 0), 0, 1), (("apply", 0, 1), 0, 0), (("mixed",), 0, 0)]
    out += [((kind, 1, h), 0, 0) for h in range(2) for kind in ("stat", "rstd")]
    out += [((kind, 1, h), c, g) for h in range(2) for kind, c, g in (("apply", 0, 1 - h), ("turn", 0.4, 0))]
    for h in range(2):
        out += [(("gated", h, m), 1.7, m == 0) for m in range(NM)]
        out += [(("hidden1", h, m), 3.4, m == 0) for m in range(NM)]
        if h == 1:
            out += [(("stat", 2, 0), 0, 0), (("rstd", 2, 0), 0, 0), (("apply", 2, 0), 0, 1), (("turn", 2, 0), 0.4, 0)]
        out += [(("hidden2", h, m), 3.4, m == 0) for m in range(NM)]
        out += [(("down", h), 3.4, 1)]
    out += [(("stat", 2, 1), 0, 1), (("rstd", 2, 1), 0, 0), (("apply", 2, 1), 0, 1), (("turn", 2, 1), 0.4, 0)]
    out += [(("proj", h), 0.8, 0) for h in range(2)]
    out += [((kind, 3, h), 0, 1 if (kind, h) == ("stat", 0) else 0) for h in range(2) for kind in ("stat", "rstd")]
    out += [((kind, 3, h), c, g) for h in range(2) for kind, c, g in (("apply", 0, 1 - h), ("turn", 0.4, 0))]
    out += [(("gates",), 3.4, 0)] + [(("recur", k), 0, 1) for k in range(5)]
    out += [(("att_out", h), 0.8, 0) for h in range(2)]
    out += [((kind, 4, h), 0, 1 if (kind, h) == ("stat", 0) else 0) for h in range(2) for kind in ("stat", "rstd")]
    out += [((kind, 4, h), c, g) for h in range(2) for kind, c, g in (("apply", 0, 1 - h), ("turn", 0.4, 0))]
    out += [(("route", 0), 0.8, 0), (("route", 1), 0, 1), (("route", 2), 0, 1), (("route", 3), 0.8, 0)]
    for h in range(2):
        out += [(("expert", h, m), 1.1, m == 0) for m in range(NM)]
        out += [(("combine", h), 3.4, 1)]
    return out


LATER = {"gated": "gate", "down": "add", "att_out": "add", "expert": "weigh", "combine": "add"}


def rest_plan(overlap):
    plan = {slot: [] for slot in SLOTS}
    late = {slot: [] for slot in SLOTS}
    at, room, used = 0, IN_ROOM, 0
    for stage, cost, gap in rest_stages():
        at += gap
        while overlap and used > sum(IN_ROOM if k < STEPS_IN else SCAN_ROOM for k in range(at + 1)):
            at += 1
        if at >= len(SLOTS) - 1:
            raise ValueError(f"no slot left at {stage}")
        used += cost
        plan[SLOTS[at]].append(stage)
        if stage[0] in LATER:
            late[SLOTS[at + 1]].append((LATER[stage[0]],) + stage)
    return {slot: late[slot] + plan[slot] for slot in SLOTS}


def bank_plan(do_scan, do_rest, plan):
    uses = []
    for slot in SLOTS:
        if do_scan:
            uses += {
                ("in", 1): [(("in_t", h), "hcm", h + 1) for h in range(2)],
                ("in", 2): [(("xs", d, h), "xs_sb", 2 * d + h + 1) for d in range(ND) for h in range(2)],
                ("in", 3): [(("z", 0, h), "z", h + 1) for h in range(2)],
                ("in", 4): [(("z", 1, h), "z", h + 3) for h in range(2)],
                ("in", 5): [(("dt", d, h), "abs_dt", 2 * d + h + 1) for d in range(ND) for h in range(2)]
                + [("bc", "c_sb", 1)],
                ("in", 7): [(("b_t", 0), "b_sb", 1), (("b_t", 1), "b_sb", 2)],
                ("out", 0): [(("y_t", d, h), "y_sum", 2 * d + h + 1) for d in range(ND) for h in range(2)],
            }.get(slot, [])
        for stage in plan[slot] if do_rest else ():
            kind, *at = stage
            if kind in LATER.values():
                continue
            h = at[0] if at else 0
            i = NM * h + at[1] + 1 if len(at) == 2 else 0
            if kind == "turn":
                n, h = at
                uses += [(stage, "xpc", h + 1) if n == 3 else (stage, "hc", {1: 0, 2: 2, 4: 4}[n] + h + 1)]
            elif kind == "route":
                uses += {0: [("logits", "lg", 1)], 3: [(("g_t", 0), "gs", 1), (("g_t", 1), "gs", 2)]}.get(h, [])
            else:
                uses += {
                    "rows": [("rows0", "wog", 1), ("rows1", "w2g", 1)],
                    "mix": [(stage, "r_norm", 4 * (h + 1))],
                    "gated": [(("gated_a", *at), "gate_a", i), (("gated_b", *at), "h0", i)],
                    "hidden1": [(stage, "g1", i)],
                    "hidden2": [(stage, "g2", i)],
                    "down": [(stage, "x_upd", 2 + h)],
                    "proj": [(stage, "r_norm", 24 + 4 * (h + 1))],
                    "gates": [((part, x), sem, x + 1) for x in range(2)
                              for part, sem in (("alpha", "tanh_a"), ("beta", "tanh_b"))],
                    "att_out": [(stage, "x_upd", 4 + h)],
                    "expert": [(("exp_h", *at), "exp_g", i), (("exp_g", *at), "gx", i)],
                    "combine": [(stage, "x_upd", 6 + h)],
                }.get(kind, [])
    return {name: (i % 3, i // 3, *(uses[i - 3][1:] if i >= 3 else (None, 0))) for i, (name, _, _) in enumerate(uses)}


SEMS = """x_in cur cur_r rest_x_in diag rows w3g wog w2g stored
p_stat p_aggr p_var p_rstd p_norm hcm pad xs_sb conv u z relu_dt abs_dt exp_dt ln_dt delta du bc_split b_sb c_sb
b_full b_spread da dbu h_done ht_full acc y_sum y
r_stat r_aggr r_var r_rstd r_norm on_g x_g2 x_upd hc gate_a h0 g1 g2
tanh_a tanh_b alpha a_shift cp cp_abs b_in bg_in c_in c_last q aq hout xpc xph q0
lg top idx gap tg wts one g_split gs exp_g gx""".split()


def build(nc, x, wts, vecs, pre, cmod, wmod, out):
    with ExitStack() as ctx:
        def sb(name, shape, dt=F32):
            return ctx.enter_context(nc.sbuf_tensor(name, shape, dt))

        def ps(name, shape):
            return ctx.enter_context(nc.psum_tensor(name, shape, F32))

        s = {n: ctx.enter_context(nc.semaphore("s_" + n)) for n in SEMS}
        bank_full = [ctx.enter_context(nc.semaphore(f"bank_full{i}")) for i in range(3)]
        pre_sem = [ctx.enter_context(nc.semaphore(f"pre{i}")) for i in range(6)]
        clear = list(s.values()) + bank_full

        W = sb("W", [P, W_COLS])
        V = sb("V", [P, V_COLS])
        ident = sb("ident", [P, P])
        ones = sb("ones", [P, P])
        mhalf = sb("mhalf", [P, NT])
        iota_e = sb("iota_e", [P, EXPERTS])
        starts = sb("starts", [P, L])
        sel_b = sb("sel_b", [SPLIT * NS, NS, P], BF16)
        sel_g = sb("sel_g", [SPLIT * EXPERTS, EXPERTS, RANK], BF16)
        w_dtx = sb("w_dtx", [P, ND, DI])
        neg_a = sb("neg_a", [P, ND, NS])
        vec = sb("vec", [P, BATCH, NVEC])
        eig_half = sb("eig_half", [P, 1])
        gate_bh = sb("gate_bh", [P, 2])
        small = sb("small", [P, 256])

        cur = sb("cur", [P, NVEC])
        cur_r = sb("cur_r", [P, NVEC])
        stat = sb("stat", [P, NT, 6])
        aggr = sb("aggr", [P, NT, 2])
        rstd = sb("rstd", [P, NT])
        var = sb("var", [P, NT])
        u = sb("u", [P, ND, L])
        zs = sb("zs", [P, ND, L])
        delta = sb("delta", [P, ND, L])
        du = sb("du", [P, ND, L])
        c_tok = sb("c_tok", [P, NT, NS])
        b_tok = sb("b_tok", [P, NT, SPLIT * NS])
        b_hi = sb("b_hi", [P, 2, NT, NS], BF16)
        b_sb = sb("b_sb", [SPLIT * NS, L], BF16)
        b_spread = sb("b_spread", [P, 2, L])
        da = sb("da", [P, RING, L])
        hst = sb("hst", [P, RING, L])
        acc = sb("acc", [P, NT, DI])
        ycm = sb("ycm", [P, ND + 1, L])
        xpad = hst[:, :, :].rearrange("p a b -> p (a b)")[:, 0:2 * (L + 4)].rearrange("p (d t) -> p d t", d=2)
        soft = da[:, 0:2, :]
        xt = da[:, 2, :].rearrange("p (j c) -> p j c", c=P)
        xn = da[:, 3, :].rearrange("p (j c) -> p j c", c=P)

        xr = sb("xr", [P, NT, P])
        rn = sb("rn", [P, NT, P])
        rstat = sb("rstat", [P, NT, 6])
        raggr = sb("raggr", [P, NT, 2])
        rrstd = sb("rrstd", [P, NT])
        rvar = sb("rvar", [P, NT])
        hc = sb("hc", [P, L])
        rows = sb("rows", [P, 2, P])
        w3g = sb("w3g", [P, NM, P])
        wog = sb("wog", [P, P])
        w2g = sb("w2g", [P, NM, P])
        ga = sb("ga", [P, HALF])
        hid = sb("hid", [P, 4, L])
        h0 = hid[:, 0:2, :].rearrange("p a (m t) -> p (a m) t", t=HALF)
        g1 = hid[:, 2:4, :].rearrange("p a (m t) -> p (a m) t", t=HALF)
        g2 = h0
        diag = hid[:, 3, 0:5 * P].rearrange("p (i c) -> p i c", c=P)
        rec = sb("rec", [P, L])
        xpc, al, ash, bb = hid[:, 0, :], hid[:, 1, :], hid[:, 2, :], hid[:, 3, :]
        qs = sb("qs", [P, L + 1])
        lg = sb("lg", [P, NT, EXPERTS])
        top = sb("top", [P, NT, 8])
        idx = sb("idx", [P, NT, 8], U32)
        idf = sb("idf", [P, NT, 8])
        gap = sb("gap", [P, NT, 2])
        oh = sb("oh", [P, 2, NT, EXPERTS])
        g_tok = sb("g_tok", [P, NT, SPLIT * EXPERTS])
        g_hi = sb("g_hi", [P, 2, NT, EXPERTS], BF16)
        g_sb = sb("g_sb", [SPLIT * EXPERTS, L], BF16)

        ht = [ps(f"ht{i}", [P, TH, DI]) for i in range(2)]
        bspr = ps("bspr", [P, HALF])
        bank = [ps(f"bank{i}", [P, HALF]) for i in range(3)]

        def w(name, n, at=0):
            return W[:, W_AT[name] + at:W_AT[name] + at + n]

        def v(name, i=0, n=1):
            return V[:, V_AT[name] + i:V_AT[name] + i + n]

        def half(ap, h):
            return ap[:, h * HALF:(h + 1) * HALF]

        ld, pv, pp, pa, pt, px = pre_sem
        wx = da[:, 0:2, :].rearrange("p a b -> p (a b)")[:, 0:2 * ND * DI].rearrange("p (a j k) -> p a j k", a=2, j=ND)
        cm = small[:, 0:2 * BATCH]
        cms = small[:, 16:16 + 2 * BATCH]
        wm = hst[:, 0:2, :].rearrange("p a b -> p (a b)")[:, 0:2 * 6 * P]
        modp = bank[0][:, 0:12 * BATCH].rearrange("p (m b) -> p m b", b=BATCH)
        mod = small[:, 32:32 + 12 * BATCH].rearrange("p (m b) -> p m b", b=BATCH)
        sgn = small[:, 128:128 + 4 * BATCH].rearrange("p (m b) -> p m b", b=BATCH)
        mag = small[:, 160:160 + 4 * BATCH].rearrange("p (m b) -> p m b", b=BATCH)
        s48 = small[0:48, 192:192 + NS]
        s24 = small[0:24, 208:208 + EXPERTS]

        with nc.Block() as block:
            @block.sync
            def _(sp):
                sp.dma_start(cm, cmod).then_inc(ld, 16)
                sp.dma_start(wm, wmod).then_inc(ld, 16)
                sp.dma_start(V[:], vecs).then_inc(ld, 16)
                sp.dma_start(wx.rearrange("p a j k -> p (a j k)"), pre).then_inc(ld, 16)
                sp.dma_start(W[:], wts).then_inc(ld, 16)
                sp.dma_start(xt, x[0].rearrange("(j p) c -> p j c", p=P)).then_inc(px, 16)
                sp.wait_ge(ld, 80)
                sp.wait_ge(px, 16)

            @block.gpsimd
            def _(pool):
                nc.gpsimd.memset(ident[:], 0.0).then_inc(pp, 1)
                nc.gpsimd.memset(ones[:], 1.0).then_inc(pp, 1)
                nc.gpsimd.memset(mhalf[:], -0.5).then_inc(pp, 1)
                nc.gpsimd.memset(starts[:], 0.0).then_inc(pp, 1)
                nc.gpsimd.iota(iota_e[:], pattern=[[1, EXPERTS]], base=0, channel_multiplier=0,
                               allow_small_or_imprecise_dtypes=True).then_inc(pp, 1)
                pool.wait_ge(pp, 5)
                nc.gpsimd.affine_select(out=ident[:], in_=ident[:], compare_op=ALU.not_equal, fill=1.0, base=0,
                                        pattern=[[-1, P]], channel_multiplier=1).then_inc(pp, 1)
                nc.gpsimd.memset(starts[:, 0:L:CHUNK], 1.0).then_inc(pp, 1)

            @block.scalar
            def _(act):
                act.wait_ge(ld, 80)
                nc.scalar.activation(cms, cm, ACT.Silu).then_inc(pa, 1)
                nc.scalar.activation(neg_a[:].rearrange("p a b -> p (a b)"), v("a_log", 0, ND * NS),
                                     ACT.Exp).then_inc(pa, 1)
                nc.scalar.activation(eig_half[:], v("eig"), ACT.Tanh).then_inc(pa, 1)

            @block.tensor
            def _(pe):
                pe.wait_ge(pa, 1)
                for m in range(12):
                    last = nc.tensor.matmul(modp[:, m, :], wm[:, m * P:(m + 1) * P],
                                            cms[:, (m // 6) * BATCH:(m // 6 + 1) * BATCH], start=True, stop=True)
                last.then_inc(pt, 1)
                for k in range(ND):
                    for j in range(ND):
                        last = nc.tensor.matmul(bank[1][:, k * DI:(k + 1) * DI], wx[:, 0, j, k * P:(k + 1) * P],
                                                wx[:, 1, j, :], start=(j == 0), stop=(j == ND - 1))
                last.then_inc(pt, 1)

            @block.vector
            def _(dve):
                steps = [0]

                def link(ins):
                    steps[0] += 1
                    ins.then_inc(pv, 1)
                    dve.wait_ge(pv, steps[0])

                dve.wait_ge(pp, 7)
                link(nc.vector.tensor_tensor(s48, ident[0:48, 0:16], ident[0:48, 16:32], ALU.add))
                link(nc.vector.tensor_tensor(s48, s48, ident[0:48, 32:48], ALU.add))
                link(nc.vector.tensor_copy(sel_b[:], s48[:, :, None].to_broadcast([48, NS, P])))
                link(nc.vector.tensor_tensor(s24, ident[0:24, 0:8], ident[0:24, 8:16], ALU.add))
                link(nc.vector.tensor_tensor(s24, s24, ident[0:24, 16:24], ALU.add))
                link(nc.vector.tensor_copy(sel_g[:], s24[:, :, None].to_broadcast([24, EXPERTS, RANK])))
                dve.wait_ge(pa, 3)
                link(nc.vector.tensor_scalar(neg_a[:], neg_a[:], -1.0, None, ALU.mult))
                link(nc.vector.tensor_scalar(eig_half[:], eig_half[:], 0.5, None, ALU.mult))
                link(nc.vector.tensor_scalar(gate_bh[:], v("gate_b", 0, 2), 0.5, None, ALU.mult))
                dve.wait_ge(pt, 2)
                link(nc.vector.tensor_copy(w_dtx[:].rearrange("p a b -> p (a b)"), bank[1][:]))
                link(nc.vector.tensor_copy(mod, modp))
                gates = mod[:, 2:12:3, :]
                link(nc.vector.tensor_scalar(sgn, gates, 0.0, 2.0, ALU.is_ge, ALU.mult))
                link(nc.vector.tensor_scalar(mag, gates, -1.0, None, ALU.mult))
                link(nc.vector.tensor_tensor(mag, mag, gates, ALU.max))
                link(nc.vector.tensor_scalar(mag, mag, 0.25, None, ALU.max))
                link(nc.vector.scalar_tensor_tensor(out=mag, in0=sgn, scalar=-1.0, in1=mag, op0=ALU.add,
                                                    op1=ALU.mult))
                for i, m in ((SA0, 0), (SB0, 3), (SA1, 6), (SB1, 9)):
                    link(nc.vector.tensor_copy(vec[:, :, i], mod[:, m, :]))
                for i, m in ((CA0, 1), (CB0, 4), (CA1, 7), (CB1, 10)):
                    link(nc.vector.tensor_scalar(vec[:, :, i], mod[:, m, :], 1.0, None, ALU.add))
                for i, g, col in ((G_LN, 0, v("ln_g")), (G_LB, 0, v("ln_b")), (G_FFN, 1, v("w3_s"))):
                    link(nc.vector.tensor_scalar(vec[:, :, i], mag[:, g, :], col, None, ALU.mult))
                link(nc.vector.tensor_scalar(vec[:, :, G_ATT], mag[:, 2, :], 0.5, None, ALU.mult))
                link(nc.vector.tensor_scalar(vec[:, :, G_MOE], mag[:, 3, :], 2.0, None, ALU.mult))

        def body(do_scan, do_rest, load_next, b):
            plan = rest_plan(do_scan)
            banks = bank_plan(do_scan, do_rest, plan)

            def full(eng, name):
                k, n, _, _ = banks[name]
                eng.wait_ge(bank_full[k], n + 1)
                return bank[k]

            def take(pe, name):
                k, _, reader, count = banks[name]
                if reader:
                    pe.wait_ge(s[reader], count)
                return bank[k]

            def filled(ins, name):
                ins.then_inc(bank_full[banks[name][0]], 1)

            with nc.Block() as block:
                @block.sync
                def _(sp):
                    if do_rest:
                        sp.dma_start(xr[:], x[bass.ds(b - 1, 1)].rearrange("o (j p) c -> p (o j) c", p=P)).then_inc(
                            s["rest_x_in"], 16)
                    if load_next:
                        sp.wait_ge(s["h_done"], 2 * NS)
                        sp.dma_start(xt, x[bass.ds(b + 1, 1)].rearrange("o (j p) c -> p (o j) c", p=P)).then_inc(
                            s["x_in"], 16)
                    if do_rest:
                        sp.wait_ge(s["x_upd"], 7)
                        sp.dma_start(out[bass.ds(b - 1, 1)].rearrange("o (j p) c -> p (o j) c", p=P), xr[:]).then_inc(
                            s["stored"], 16)
                        sp.wait_ge(s["stored"], 16)
                    if load_next:
                        sp.wait_ge(s["x_in"], 16)

                @block.tensor
                def _(pe):
                    def turn(name, src, sem, count):
                        pe.wait_ge(sem, count)
                        o = take(pe, name)
                        for jj in range(TH):
                            last = nc.tensor.transpose(o[:, jj * P:(jj + 1) * P], src(jj), ident[:])
                        filled(last, name)

                    def mixer_in(k):
                        if k == 1:
                            for h in range(2):
                                turn(("in_t", h), lambda jj: xn[:, h * TH + jj, :], s["p_norm"], 4 * (h + 1))
                        elif k in (2, 3, 4):
                            if k == 2:
                                pe.wait_ge(s["hcm"], 2)
                            uses = [("xs", d, h) for d in range(ND) for h in range(2)] if k == 2 else \
                                [("z", k - 3, h) for h in range(2)]
                            for name in uses:
                                part, d, h = name
                                at = (DI if part == "z" else 0) + d * P
                                o = take(pe, name)
                                filled(nc.tensor.matmul(o[:], w("w_in", P, at), half(ycm[:, ND, :], h), start=True,
                                                        stop=True), name)
                        elif k == 5:
                            pe.wait_ge(s["u"], 2)
                            for m in range(ND):
                                for h in range(2):
                                    o = take(pe, ("dt", m, h))
                                    for i in range(ND):
                                        last = nc.tensor.matmul(o[:], w_dtx[:, i, m * P:(m + 1) * P],
                                                                half(u[:, i, :], h), start=(i == 0), stop=(i == ND - 1))
                                    filled(last, ("dt", m, h))
                            o = take(pe, "bc")
                            for j in range(NT):
                                for i in range(ND):
                                    last = nc.tensor.matmul(o[:, j * 2 * NS:(j + 1) * 2 * NS],
                                                            u[:, i, j * P:(j + 1) * P],
                                                            w("w_bc", 2 * NS, i * 2 * NS), start=(i == 0),
                                                            stop=(i == ND - 1))
                            filled(last, "bc")
                        elif k == 7:
                            pe.wait_ge(s["bc_split"], 5)
                            for h in range(2):
                                o = take(pe, ("b_t", h))
                                for jj in range(TH):
                                    last = nc.tensor.transpose(o[0:SPLIT * NS, jj * P:(jj + 1) * P],
                                                               b_tok[:, h * TH + jj, :], ident[:])
                                filled(last, ("b_t", h))

                    def scan(t):
                        n, c = t // 2, t % 2
                        if n + 3 < NS:
                            i = 2 * (n + 3) + c
                            if i == 0:
                                pe.wait_ge(s["b_sb"], 2)
                            else:
                                pe.wait_ge(s["b_spread"], i)
                            nc.tensor.matmul(bspr[:], sel_b[:, n + 3, :], half(b_sb[:], c), start=True,
                                             stop=True).then_inc(s["b_full"], 1)
                        if 0 <= n < NS:
                            pe.wait_ge(s["h_done"], 2 * n + 2)
                            if n >= 1:
                                pe.wait_ge(s["acc"], TH * (2 * n - 1 + c))
                            for jj in range(TH):
                                for d in range(ND):
                                    at = (c * TH + jj) * P
                                    last = nc.tensor.transpose(ht[c][:, jj, d * P:(d + 1) * P],
                                                               hst[:, (2 * n + d) % RING, at:at + P], ident[:])
                            last.then_inc(s["ht_full"], 1)

                    def rest(stage):
                        kind = stage[0]
                        if kind == "rows":
                            pe.wait_ge(s["diag"], 5)
                            for name, a, n in (("rows0", 0, 4), ("rows1", 4, 1)):
                                o = take(pe, name)
                                for i in range(n):
                                    last = nc.tensor.matmul(o[:, i * P:(i + 1) * P], ones[:], diag[:, a + i, :],
                                                            start=True, stop=True)
                                filled(last, name)
                        elif kind == "mix":
                            h = stage[1]
                            o = take(pe, stage)
                            for jj in range(TH):
                                t = (h * TH + jj) * P
                                for k in range(ND + 1):
                                    rhs = w("w_out", P, k * P) if k < ND else ident[:]
                                    last = nc.tensor.matmul(o[:, jj * P:(jj + 1) * P], ycm[:, k, t:t + P], rhs,
                                                            start=(k == 0), stop=(k == ND))
                            filled(last, stage)
                        elif kind == "turn":
                            n, h = stage[1:]
                            turn(stage, lambda jj: rn[:, h * TH + jj, :], s["r_norm"], 8 * n + 4 * (h + 1))
                        elif kind == "gated":
                            h, m = stage[1:]
                            pe.wait_ge(s["hc"], 1 + h)
                            for part, wt in (("gated_a", "w1"), ("gated_b", "w2")):
                                o = take(pe, (part, h, m))
                                filled(nc.tensor.matmul(o[:], w(wt, P, m * P), half(hc[:], h), start=True, stop=True),
                                       (part, h, m))
                        elif kind in ("hidden1", "hidden2"):
                            h, m = stage[1:]
                            wt, src, sem = ("h1", h0, s["h0"]) if kind == "hidden1" else ("h2", g1, s["g1"])
                            o = take(pe, stage)
                            for k in range(NM):
                                if m == 0:
                                    pe.wait_ge(sem, NM * h + k + 1)
                                last = nc.tensor.matmul(o[:], w(wt, P, k * HID + m * P), src[:, k, :], start=(k == 0),
                                                        stop=(k == NM - 1))
                            filled(last, stage)
                        elif kind == "down":
                            h = stage[1]
                            pe.wait_ge(s["g2"], NM * (h + 1))
                            pe.wait_ge(s["w3g"], 1)
                            o = take(pe, stage)
                            for jj in range(TH):
                                for k in range(NM):
                                    last = nc.tensor.matmul(o[:, jj * P:(jj + 1) * P], g2[:, k, jj * P:(jj + 1) * P],
                                                            w3g[:, k, :], start=(k == 0), stop=(k == NM - 1))
                            filled(last, stage)
                        elif kind == "proj":
                            h = stage[1]
                            pe.wait_ge(s["hc"], 3 + h)
                            o = take(pe, stage)
                            for jj in range(TH):
                                t = (h * TH + jj) * P
                                last = nc.tensor.matmul(o[:, jj * P:(jj + 1) * P], hc[:, t:t + P], w("b_in", P),
                                                        start=True, stop=True)
                            filled(last, stage)
                        elif kind == "gates":
                            pe.wait_ge(s["xpc"], 2)
                            for h in range(2):
                                for i, part in enumerate(("alpha", "beta")):
                                    o = take(pe, (part, h))
                                    filled(nc.tensor.matmul(o[:], w("b_gate", P, i * P), half(xpc, h), start=True,
                                                            stop=True), (part, h))
                        elif kind == "att_out":
                            pe.wait_ge(s["hout"], 1)
                            pe.wait_ge(s["wog"], 1)
                            h = stage[1]
                            o = take(pe, stage)
                            for jj in range(TH):
                                t = (h * TH + jj) * P
                                last = nc.tensor.matmul(o[:, jj * P:(jj + 1) * P], rec[:, t:t + P], wog[:],
                                                        start=True, stop=True)
                            filled(last, stage)
                        elif stage == ("route", 0):
                            pe.wait_ge(s["hc"], 6)
                            o = take(pe, "logits")
                            for j in range(NT):
                                last = nc.tensor.matmul(o[:, j * EXPERTS:(j + 1) * EXPERTS], hc[:, j * P:(j + 1) * P],
                                                        w("e_gate", EXPERTS), start=True, stop=True)
                            filled(last, "logits")
                        elif stage == ("route", 3):
                            pe.wait_ge(s["g_split"], 5)
                            for h in range(2):
                                o = take(pe, ("g_t", h))
                                for jj in range(TH):
                                    last = nc.tensor.transpose(o[0:SPLIT * EXPERTS, jj * P:(jj + 1) * P],
                                                               g_tok[:, h * TH + jj, :], ident[:])
                                filled(last, ("g_t", h))
                        elif kind == "expert":
                            h, m = stage[1:]
                            pe.wait_ge(s["gs"], 2)
                            o = take(pe, ("exp_h", h, m))
                            filled(nc.tensor.matmul(o[:], w("e1", P, m * P), half(hc[:], h), start=True, stop=True),
                                   ("exp_h", h, m))
                            o = take(pe, ("exp_g", h, m))
                            filled(nc.tensor.matmul(o[:], sel_g[:, 2 * m:2 * m + 2, :].rearrange("p a b -> p (a b)"),
                                                    half(g_sb[:], h), start=True, stop=True), ("exp_g", h, m))
                        elif kind == "combine":
                            h = stage[1]
                            pe.wait_ge(s["gx"], NM * (h + 1))
                            pe.wait_ge(s["w2g"], 1)
                            o = take(pe, stage)
                            for jj in range(TH):
                                for k in range(NM):
                                    last = nc.tensor.matmul(o[:, jj * P:(jj + 1) * P], h0[:, k, jj * P:(jj + 1) * P],
                                                            w2g[:, k, :], start=(k == 0), stop=(k == NM - 1))
                            filled(last, stage)

                    def mixer_end(_):
                        pe.wait_ge(s["acc"], NT * NS)
                        for d in range(ND):
                            for h in range(2):
                                o = take(pe, ("y_t", d, h))
                                for jj in range(TH):
                                    last = nc.tensor.transpose(o[:, jj * P:(jj + 1) * P],
                                                               acc[:, h * TH + jj, d * P:(d + 1) * P], ident[:])
                                filled(last, ("y_t", d, h))

                    for slot in SLOTS:
                        if do_scan:
                            step = {"in": mixer_in, "scan": scan, "out": mixer_end}[slot[0]]
                            step(slot[1])
                        if do_rest:
                            for stage in plan[slot]:
                                rest(stage)

                @block.scalar
                def _(act):
                    def mixer_in(k):
                        if k == 1:
                            act.wait_ge(s["cur"], 1)
                            if do_rest:
                                full(act, ("mix", 1))
                            for h in range(2):
                                o = full(act, ("in_t", h))
                                nc.scalar.activation(half(ycm[:, ND, :], h), o[:], ACT.Identity,
                                                     bias=cur[:, SA0:SA0 + 1],
                                                     scale=cur[:, CA0:CA0 + 1]).then_inc(s["hcm"], 1)
                        elif k == 2:
                            for d in range(ND):
                                for h in range(2):
                                    o = full(act, ("xs", d, h))
                                    at = TAPS - 1 + h * HALF
                                    nc.scalar.activation(xpad[:, d, at:at + HALF], o[:], ACT.Copy).then_inc(
                                        s["xs_sb"], 1)
                        elif k in (3, 4):
                            for h in range(2):
                                o = full(act, ("z", k - 3, h))
                                nc.scalar.activation(half(zs[:, k - 3, :], h), o[:], ACT.Silu).then_inc(s["z"], 1)
                        if k in (4, 5):
                            d = k - 4
                            act.wait_ge(s["conv"], TAPS * (d + 1))
                            nc.scalar.activation(u[:, d, :], u[:, d, :], ACT.Silu,
                                                 bias=v("conv_b", d)).then_inc(s["u"], 1)
                        if k == 5:
                            for d in range(ND):
                                for h in range(2):
                                    o = full(act, ("dt", d, h))
                                    nc.scalar.activation(half(delta[:, d, :], h), o[:], ACT.Relu,
                                                         bias=v("b_dt", d)).then_inc(s["relu_dt"], 1)
                                    nc.scalar.activation(half(soft[:, d, :], h), o[:], ACT.Abs,
                                                         bias=v("b_dt", d)).then_inc(s["abs_dt"], 1)
                        elif k == 6:
                            act.wait_ge(s["abs_dt"], 4)
                            nc.scalar.activation(soft, soft, ACT.Exp, scale=-1.0).then_inc(s["exp_dt"], 1)
                            act.wait_ge(s["exp_dt"], 1)
                            nc.scalar.activation(soft, soft, ACT.Ln, bias=1.0).then_inc(s["ln_dt"], 1)
                        elif k == 7:
                            for h in range(2):
                                o = full(act, ("b_t", h))
                                nc.scalar.activation(half(b_sb[:], h), o[0:SPLIT * NS, :], ACT.Copy).then_inc(
                                    s["b_sb"], 1)

                    def scan(t):
                        n, c = t // 2, t % 2
                        if n + 3 < NS:
                            m = n + 3
                            act.wait_ge(s["b_full"], 2 * m + c + 1)
                            if m >= 2:
                                act.wait_ge(s["dbu"], 2 * m - 2)
                            nc.scalar.activation(half(b_spread[:, m % 2, :], c), bspr[:], ACT.Copy).then_inc(
                                s["b_spread"], 1)
                        if t % EXPS == 0:
                            for i in range(t + 4, min(t + 4 + EXPS, 2 * NS)):
                                act.wait_ge(s["delta"], 2)
                                if i >= RING:
                                    act.wait_ge(s["h_done"], i - RING + 1)
                                nc.scalar.activation(da[:, i % RING, :], delta[:, i % 2, :], ACT.Exp,
                                                     scale=neg_a[:, i % 2, i // 2:i // 2 + 1]).then_inc(s["da"], 1)

                    def mixer_end(_):
                        pass

                    def rest(stage):
                        kind = stage[0]
                        if kind == "turn":
                            n, h = stage[1:]
                            o = full(act, stage)
                            if n == 3:
                                nc.scalar.activation(half(xpc, h), o[:], ACT.Identity, bias=v("l_b"),
                                                     scale=v("l_g")).then_inc(s["xpc"], 1)
                            else:
                                bias, scale = {1: (SB0, CB0), 2: (SA1, CA1), 4: (SB1, CB1)}[n]
                                nc.scalar.activation(half(hc[:], h), o[:], ACT.Identity, bias=cur_r[:, bias:bias + 1],
                                                     scale=cur_r[:, scale:scale + 1]).then_inc(s["hc"], 1)
                        elif kind == "gated":
                            h, m = stage[1:]
                            o = full(act, ("gated_a", h, m))
                            if NM * h + m:
                                act.wait_ge(s["h0"], NM * h + m)
                            nc.scalar.activation(ga[:], o[:], ACT.Silu, scale=v("w1_s", m)).then_inc(s["gate_a"], 1)
                        elif kind in ("hidden1", "hidden2"):
                            h, m = stage[1:]
                            dst, col, sem = (g1, "h1_s", s["g1"]) if kind == "hidden1" else (g2, "h2_s", s["g2"])
                            o = full(act, stage)
                            nc.scalar.activation(dst[:, m, :], o[:], ACT.Gelu, scale=v(col, m)).then_inc(sem, 1)
                        elif kind == "gates":
                            for h in range(2):
                                for i, (part, dst, sem) in enumerate((("alpha", al, s["tanh_a"]), ("beta", bb, s["tanh_b"]))):
                                    o = full(act, (part, h))
                                    nc.scalar.activation(half(dst, h), o[:], ACT.Tanh, bias=gate_bh[:, i:i + 1],
                                                               scale=0.5).then_inc(sem, 1)
                        elif stage == ("recur", 2):
                            act.wait_ge(s["cp"], 1)
                            nc.scalar.activation(rec[:], rec[:], ACT.Abs).then_inc(s["cp_abs"], 1)
                        elif stage == ("route", 1):
                            act.wait_ge(s["gap"], 1)
                            nc.scalar.activation(gap[:, :, 0:1], gap[:, :, 0:1], ACT.Tanh, scale=0.5).then_inc(s["tg"], 1)
                        elif stage == ("route", 3):
                            for h in range(2):
                                o = full(act, ("g_t", h))
                                nc.scalar.activation(half(g_sb[:], h), o[0:SPLIT * EXPERTS, :], ACT.Copy).then_inc(s["gs"], 1)
                        elif kind == "expert":
                            h, m = stage[1:]
                            o = full(act, ("exp_h", h, m))
                            if h == 1 and m == 0:
                                act.wait_ge(s["x_upd"], 6)
                            nc.scalar.activation(h0[:, m, :], o[:], ACT.Gelu).then_inc(s["exp_g"], 1)

                    for slot in SLOTS:
                        if do_scan:
                            step = {"in": mixer_in, "scan": scan, "out": mixer_end}[slot[0]]
                            step(slot[1])
                        if do_rest:
                            for stage in plan[slot]:
                                rest(stage)

                @block.gpsimd
                def _(pool):
                    def inv_std(n, h, ag, vr, rs, s_ag, s_vr, s_rs):
                        j = slice(h * TH, (h + 1) * TH)
                        pool.wait_ge(s_ag, 8 * n + 4 * (h + 1))
                        nc.gpsimd.tensor_scalar(vr[:, j], ag[:, j, 1], EPS, None, ALU.add).then_inc(s_vr, 1)
                        pool.wait_ge(s_vr, 2 * n + h + 1)
                        nc.gpsimd.tensor_tensor(rs[:, j], vr[:, j], mhalf[:, j], ALU.pow).then_inc(s_rs, 1)

                    def mixer_in(k):
                        if k == 0:
                            for h in range(2):
                                inv_std(0, h, aggr, var, rstd, s["p_aggr"], s["p_var"], s["p_rstd"])
                        elif k == 7:
                            for d in range(ND):
                                pool.wait_ge(s["delta"], d + 1)
                                nc.gpsimd.tensor_tensor(du[:, d, :], delta[:, d, :], u[:, d, :], ALU.mult).then_inc(
                                    s["du"], 1)
                            pool.wait_ge(s["du"], 2)

                    def scan(t):
                        n, c = t // 2, t % 2
                        if 0 <= n + 2 < NS:
                            i = 2 * (n + 2) + c
                            pool.wait_ge(s["b_spread"], 2 * (n + 2) + 2)
                            if i >= RING:
                                pool.wait_ge(s["ht_full"], 2 * ((i - RING) // 2) + 2)
                            nc.gpsimd.tensor_tensor(hst[:, i % RING, :], du[:, c, :], b_spread[:, (n + 2) % 2, :],
                                                    ALU.mult).then_inc(s["dbu"], 1)

                    def mixer_end(_):
                        pass

                    def rest(stage):
                        if stage[0] == "rstd":
                            inv_std(*stage[1:], raggr, rvar, rrstd, s["r_aggr"], s["r_var"], s["r_rstd"])

                    for slot in SLOTS:
                        if do_scan:
                            step = {"in": mixer_in, "scan": scan, "out": mixer_end}[slot[0]]
                            step(slot[1])
                        if do_rest:
                            for stage in plan[slot]:
                                rest(stage)

                @block.vector
                def _(dve):
                    def statistics(n, h, src, st, ag, s_st, s_ag):
                        for jj in range(TH):
                            nc.vector.bn_stats(st[:, h * TH + jj, :], src(jj)).then_inc(s_st, 1)
                        dve.wait_ge(s_st, 8 * n + 4 * (h + 1))
                        for jj in range(TH):
                            nc.vector.bn_aggr(ag[:, h * TH + jj, :], st[:, h * TH + jj, :]).then_inc(s_ag, 1)

                    def normalize(n, h, src, ag, rs, dst, s_ag, s_rs, s_nm):
                        dve.wait_ge(s_ag, 8 * n + 4 * (h + 1))
                        dve.wait_ge(s_rs, 2 * n + h + 1)
                        for jj in range(TH):
                            j = h * TH + jj
                            nc.vector.tensor_scalar(dst[:, j, :], src(jj), ag[:, j, 0:1], rs[:, j:j + 1], ALU.subtract,
                                                    ALU.mult).then_inc(s_nm, 1)

                    def norm_source(n, h):
                        if n in (0, 3):
                            o = full(dve, ("mix" if n == 0 else "proj", h))
                            return lambda jj: o[:, jj * P:(jj + 1) * P]
                        return lambda jj: xr[:, h * TH + jj, :]

                    def add_half(name, h, count):
                        o = full(dve, name)
                        dve.wait_ge(s["x_upd"], count)
                        xh = xr[:, h * TH:(h + 1) * TH, :].rearrange("p j c -> p (j c)")
                        nc.vector.tensor_tensor(xh, o[:], xh, ALU.add).then_inc(s["x_upd"], 1)

                    def rows_out():
                        nc.vector.tensor_copy(cur_r[:], vec[:, bass.ds(b - 1, 1), :].rearrange("p o n -> p (o n)")
                                              ).then_inc(s["cur_r"], 1)
                        dve.wait_ge(s["cur_r"], 1)
                        for i, col in enumerate((G_LN, G_LB, G_FFN, G_ATT, G_MOE)):
                            nc.vector.tensor_scalar(diag[:, i, :], ident[:], cur_r[:, col:col + 1], None,
                                                    ALU.mult).then_inc(s["diag"], 1)
                        o = full(dve, "rows0")
                        nc.vector.tensor_copy(rows[:].rearrange("p a c -> p (a c)"), o[:, 0:2 * P]).then_inc(
                            s["rows"], 1)
                        nc.vector.tensor_tensor(w3g[:], w("w3", NM * P).rearrange("p (k c) -> p k c", k=NM),
                                                o[:, None, 2 * P:3 * P].to_broadcast([P, NM, P]), ALU.mult
                                                ).then_inc(s["w3g"], 1)
                        nc.vector.tensor_tensor(wog[:], w("b_out", P), o[:, 3 * P:4 * P], ALU.mult).then_inc(
                            s["wog"], 1)
                        o = full(dve, "rows1")
                        nc.vector.tensor_tensor(w2g[:], w("e2", NM * P).rearrange("p (k c) -> p k c", k=NM),
                                                o[:, None, 0:P].to_broadcast([P, NM, P]), ALU.mult).then_inc(
                            s["w2g"], 1)

                    def mixed():
                        dve.wait_ge(s["rest_x_in"], 16)
                        dve.wait_ge(s["rows"], 1)
                        nc.vector.tensor_tensor(xr[:], xr[:], rows[:, None, 1, :].to_broadcast([P, NT, P]),
                                                ALU.add).then_inc(s["x_g2"], 1)
                        dve.wait_ge(s["r_norm"], 8)
                        nc.vector.tensor_tensor(rn[:], rn[:], rows[:, None, 0, :].to_broadcast([P, NT, P]),
                                                ALU.mult).then_inc(s["on_g"], 1)
                        dve.wait_ge(s["on_g"], 1)
                        dve.wait_ge(s["x_g2"], 1)
                        nc.vector.tensor_tensor(xr[:], xr[:], rn[:], ALU.add).then_inc(s["x_upd"], 1)

                    def split(dst, hi, n, parts, sem):
                        for i in range(parts - 1):
                            a, c = dst[:, :, i * n:(i + 1) * n], dst[:, :, (i + 1) * n:(i + 2) * n]
                            dve.wait_ge(sem, 2 * i + 1)
                            nc.vector.tensor_copy(hi[:, i, :, :], a).then_inc(sem, 1)
                            dve.wait_ge(sem, 2 * i + 2)
                            nc.vector.tensor_tensor(c, a, hi[:, i, :, :], ALU.subtract).then_inc(sem, 1)

                    def mixer_in(k):
                        if k == 0:
                            nc.vector.tensor_copy(cur[:], vec[:, bass.ds(b, 1), :].rearrange("p o n -> p (o n)")
                                                  ).then_inc(s["cur"], 1)
                            nc.vector.memset(xpad[:, :, 0:TAPS - 1], 0.0).then_inc(s["pad"], 1)
                            for h in range(2):
                                statistics(0, h, lambda jj: xt[:, h * TH + jj, :], stat, aggr, s["p_stat"], s["p_aggr"])
                        elif k == 1:
                            for h in range(2):
                                normalize(0, h, lambda jj: xt[:, h * TH + jj, :], aggr, rstd, xn, s["p_aggr"],
                                          s["p_rstd"], s["p_norm"])
                        elif k in (3, 4):
                            d = k - 3
                            dve.wait_ge(s["pad"], 1)
                            dve.wait_ge(s["xs_sb"], 2 * (d + 1))
                            for i in range(TAPS):
                                tap = v("conv_w", d * TAPS + i)
                                if i == 0:
                                    ins = nc.vector.tensor_scalar(u[:, d, :], xpad[:, d, 0:L], tap, None, ALU.mult)
                                else:
                                    dve.wait_ge(s["conv"], TAPS * d + i)
                                    ins = nc.vector.scalar_tensor_tensor(out=u[:, d, :], in0=xpad[:, d, i:i + L],
                                                                         scalar=tap, in1=u[:, d, :], op0=ALU.mult,
                                                                         op1=ALU.add)
                                ins.then_inc(s["conv"], 1)
                        elif k == 6:
                            o = full(dve, "bc")[:, 0:NT * 2 * NS].rearrange("p (j n) -> p j n", n=2 * NS)
                            nc.vector.tensor_copy(b_tok[:, :, 0:NS], o[:, :, 0:NS]).then_inc(s["bc_split"], 1)
                            nc.vector.tensor_copy(c_tok[:], o[:, :, NS:2 * NS]).then_inc(s["c_sb"], 1)
                            split(b_tok, b_hi, NS, SPLIT, s["bc_split"])
                        elif k == 7:
                            dve.wait_ge(s["ln_dt"], 1)
                            for d in range(ND):
                                nc.vector.tensor_tensor(delta[:, d, :], delta[:, d, :], soft[:, d, :],
                                                        ALU.add).then_inc(s["delta"], 1)

                    def scan(t):
                        n, c = t // 2, t % 2
                        if 0 <= n + 1 < NS:
                            i = 2 * (n + 1) + c
                            dve.wait_ge(s["da"], i + 1)
                            dve.wait_ge(s["dbu"], i + 1)
                            nc.vector.tensor_tensor_scan(hst[:, i % RING, :], da[:, i % RING, :], hst[:, i % RING, :],
                                                         0.0, ALU.mult, ALU.add).then_inc(s["h_done"], 1)
                        if t >= 1:
                            n, c = (t - 1) // 2, (t - 1) % 2
                            dve.wait_ge(s["ht_full"], t)
                            if n == 0:
                                dve.wait_ge(s["c_sb"], 1)
                            else:
                                dve.wait_ge(s["acc"], TH * (2 * n - 1 + c))
                            for jj in range(TH):
                                j = c * TH + jj
                                if n == 0:
                                    ins = nc.vector.tensor_scalar(acc[:, j, :], ht[c][:, jj, :], c_tok[:, j, 0:1], None,
                                                                  ALU.mult)
                                else:
                                    ins = nc.vector.scalar_tensor_tensor(out=acc[:, j, :], in0=ht[c][:, jj, :],
                                                                         scalar=c_tok[:, j, n:n + 1], in1=acc[:, j, :],
                                                                         op0=ALU.mult, op1=ALU.add)
                                ins.then_inc(s["acc"], 1)

                    def rest(stage):
                        kind = stage[0]
                        if kind == "rows":
                            rows_out()
                        elif kind == "mixed":
                            mixed()
                        elif kind == "stat":
                            n, h = stage[1:]
                            if n in (1, 2, 4):
                                dve.wait_ge(s["x_upd"], {1: 1, 2: 2 + h, 4: 4 + h}[n])
                            statistics(n, h, norm_source(n, h), rstat, raggr, s["r_stat"], s["r_aggr"])
                        elif kind == "apply":
                            n, h = stage[1:]
                            normalize(n, h, norm_source(n, h), raggr, rrstd, rn, s["r_aggr"], s["r_rstd"], s["r_norm"])
                        elif kind == "gate":
                            h, m = stage[2:]
                            o = full(dve, ("gated_b", h, m))
                            dve.wait_ge(s["gate_a"], NM * h + m + 1)
                            nc.vector.scalar_tensor_tensor(out=h0[:, m, :], in0=o[:], scalar=v("w2_s", m), in1=ga[:],
                                                           op0=ALU.mult, op1=ALU.mult).then_inc(s["h0"], 1)
                        elif kind == "add":
                            add_half(stage[1:], stage[2], stage[2] + {"down": 1, "att_out": 3, "combine": 5}[stage[1]])
                        elif stage == ("recur", 0):
                            dve.wait_ge(s["tanh_a"], 2)
                            nc.vector.tensor_scalar(al, al, eig_half[:], eig_half[:], ALU.mult,
                                                    ALU.add).then_inc(s["alpha"], 1)
                            dve.wait_ge(s["alpha"], 1)
                            nc.vector.tensor_copy(ash[:, 1:L], al[:, 0:L - 1]).then_inc(s["a_shift"], 1)
                            dve.wait_ge(s["a_shift"], 1)
                            nc.vector.memset(ash[:, 0:L:CHUNK], 0.0).then_inc(s["a_shift"], 1)
                        elif stage == ("recur", 1):
                            dve.wait_ge(s["tanh_b"], 2)
                            nc.vector.scalar_tensor_tensor(out=bb, in0=bb, scalar=1.0, in1=xpc, op0=ALU.add,
                                                           op1=ALU.mult).then_inc(s["b_in"], 1)
                            dve.wait_ge(s["a_shift"], 2)
                            nc.vector.tensor_tensor_scan(rec[:], ash, starts[:], 0.0, ALU.mult,
                                                         ALU.add).then_inc(s["cp"], 1)
                        elif stage == ("recur", 3):
                            dve.wait_ge(s["cp_abs"], 1)
                            dve.wait_ge(s["b_in"], 1)
                            nc.vector.scalar_tensor_tensor(out=rec[:], in0=rec[:], scalar=1e-8, in1=bb, op0=ALU.is_gt,
                                                           op1=ALU.mult).then_inc(s["bg_in"], 1)
                            dve.wait_ge(s["bg_in"], 1)
                            nc.vector.tensor_tensor(rec[:], rec[:], al, ALU.mult).then_inc(s["c_in"], 1)
                            dve.wait_ge(s["c_in"], 1)
                            nc.vector.tensor_copy(rec[:, CHUNK - 1:L:CHUNK], bb[:, CHUNK - 1:L:CHUNK]).then_inc(s["c_last"], 1)
                        elif stage == ("recur", 4):
                            nc.vector.memset(qs[:, 0:1], 0.0).then_inc(s["q0"], 1)
                            dve.wait_ge(s["c_last"], 1)
                            nc.vector.tensor_tensor_scan(qs[:, 1:L + 1], al, rec[:], 0.0, ALU.mult,
                                                         ALU.add).then_inc(s["q"], 1)
                            dve.wait_ge(s["q"], 1)
                            dve.wait_ge(s["q0"], 1)
                            nc.vector.tensor_tensor(rec[:], al, qs[:, 0:L], ALU.mult).then_inc(s["aq"], 1)
                            dve.wait_ge(s["aq"], 1)
                            nc.vector.tensor_tensor(rec[:], rec[:], bb, ALU.add).then_inc(s["hout"], 1)
                        elif stage == ("route", 1):
                            o = full(dve, "logits")[:, 0:NT * EXPERTS].rearrange("p (j e) -> p j e", e=EXPERTS)
                            nc.vector.tensor_tensor(lg[:], o, v("bg", 0, EXPERTS)[:, None, :].to_broadcast(
                                [P, NT, EXPERTS]), ALU.add).then_inc(s["lg"], 1)
                            dve.wait_ge(s["lg"], 1)
                            for j in range(NT):
                                nc.vector.max(top[:, j, :], lg[:, j, :]).then_inc(s["top"], 1)
                            dve.wait_ge(s["top"], NT)
                            for j in range(NT):
                                nc.vector.max_index(idx[:, j, :], top[:, j, :], lg[:, j, :]).then_inc(s["idx"], 1)
                            nc.vector.tensor_tensor(gap[:, :, 0:1], top[:, :, 0:1], top[:, :, 1:2],
                                                    ALU.subtract).then_inc(s["gap"], 1)
                            dve.wait_ge(s["idx"], NT)
                            nc.vector.tensor_copy(idf[:], idx[:]).then_inc(s["one"], 1)
                            dve.wait_ge(s["one"], 1)
                            for i in range(2):
                                nc.vector.tensor_tensor(oh[:, i, :, :], iota_e[:, None, :].to_broadcast([P, NT, EXPERTS]),
                                                        idf[:, :, i:i + 1].to_broadcast([P, NT, EXPERTS]),
                                                        ALU.is_equal).then_inc(s["one"], 1)
                        elif stage == ("route", 2):
                            dve.wait_ge(s["tg"], 1)
                            nc.vector.tensor_scalar(gap[:, :, 1:2], gap[:, :, 0:1], -0.5, 0.5, ALU.mult,
                                                    ALU.add).then_inc(s["wts"], 1)
                            dve.wait_ge(s["wts"], 1)
                            nc.vector.tensor_scalar(gap[:, :, 0:1], gap[:, :, 0:1], 0.5, 0.5, ALU.mult,
                                                    ALU.add).then_inc(s["wts"], 1)
                            dve.wait_ge(s["wts"], 2)
                            dve.wait_ge(s["one"], 3)
                            for i in range(2):
                                nc.vector.tensor_tensor(oh[:, i, :, :], oh[:, i, :, :],
                                                        gap[:, :, i:i + 1].to_broadcast([P, NT, EXPERTS]),
                                                        ALU.mult).then_inc(s["one"], 1)
                            dve.wait_ge(s["one"], 5)
                            nc.vector.tensor_tensor(g_tok[:, :, 0:EXPERTS], oh[:, 0, :, :], oh[:, 1, :, :],
                                                    ALU.add).then_inc(s["g_split"], 1)
                            split(g_tok, g_hi, EXPERTS, SPLIT, s["g_split"])
                        elif kind == "weigh":
                            h, m = stage[2:]
                            o = full(dve, ("exp_g", h, m))
                            dve.wait_ge(s["exp_g"], NM * h + m + 1)
                            nc.vector.tensor_tensor(h0[:, m, :], o[:], h0[:, m, :], ALU.mult).then_inc(s["gx"], 1)

                    def mixer_end(_):
                        dve.wait_ge(s["z"], 4)
                        for d in range(ND):
                            for h in range(2):
                                o = full(dve, ("y_t", d, h))
                                i = 2 * d + h + 1
                                nc.vector.scalar_tensor_tensor(out=half(ycm[:, d, :], h), in0=half(u[:, d, :], h),
                                                               scalar=v("d", d), in1=o[:], op0=ALU.mult,
                                                               op1=ALU.add).then_inc(s["y_sum"], 1)
                                dve.wait_ge(s["y_sum"], i)
                                nc.vector.tensor_tensor(half(ycm[:, d, :], h), half(ycm[:, d, :], h),
                                                        half(zs[:, d, :], h), ALU.mult).then_inc(s["y"], 1)

                    for slot in SLOTS:
                        if do_scan:
                            step = {"in": mixer_in, "scan": scan, "out": mixer_end}[slot[0]]
                            step(slot[1])
                        if do_rest:
                            for stage in plan[slot]:
                                rest(stage)

            for q in clear:
                nc.gpsimd.sem_clear(q)
            nc.all_engine_barrier(sem_only=True)

        body(True, False, True, 0)
        with nc.Fori(1, BATCH - 1) as b:
            body(True, True, True, b)
        body(True, True, False, BATCH - 1)
        body(False, True, False, BATCH)


def kernel(**inputs):
    import numpy as np
    import concourse.bacc as bacc
    from concourse.bass_utils import run_bass_kernel_spmd

    a = {k: np.asarray(t) for k, t in inputs.items()}

    def rows_to(t):
        n = t.shape[0] // P
        return np.ascontiguousarray(t.reshape(n, P, -1).transpose(1, 0, 2).reshape(P, -1))

    wx = a["L0_attn_W_x"]
    gate = a["L1_attn_W_gate"]
    spread = lambda t: np.repeat(t, P // HEADS, axis=0)
    wts = np.concatenate([
        a["L0_attn_W_in"].T, rows_to(wx[DI:].T), rows_to(a["L0_attn_W_out"].T), a["L0_ffn_w1_w"].T,
        a["L0_ffn_w2_w"].T, rows_to(a["L0_ffn_h1_w"].T), rows_to(a["L0_ffn_h2_w"].T), rows_to(a["L0_ffn_w3_w"].T),
        a["L1_attn_W_in"].T, spread(gate[:HEADS]).T, spread(gate[HEADS:]).T, a["L1_attn_W_out"].T,
        a["L1_ffn_W1"].reshape(EXPERTS * RANK, P).T, rows_to(a["L1_ffn_W2"].transpose(0, 2, 1).reshape(-1, P)),
        a["L1_ffn_Wg"].T], axis=1)
    col = lambda t: rows_to(t.reshape(-1, 1))
    vecs = np.concatenate([
        rows_to(a["L0_attn_conv_w"].reshape(DI, TAPS)), col(a["L0_attn_conv_b"]), col(a["L0_attn_b_dt"]),
        rows_to(a["L0_attn_A_log"]), col(a["L0_attn_D"]), col(a["L0_attn_ln_g"]), col(a["L0_attn_ln_b"]),
        col(a["L0_ffn_w1_s"]), col(a["L0_ffn_w2_s"]), col(a["L0_ffn_h1_s"]), col(a["L0_ffn_h2_s"]),
        col(a["L0_ffn_w3_s"]), col(a["L1_attn_ln_g"]), col(a["L1_attn_ln_b"]),
        col(spread(a["L1_attn_b_gate"][:HEADS])), col(spread(a["L1_attn_b_gate"][HEADS:])),
        col(spread(a["L1_attn_eig_raw"])), np.broadcast_to(a["L1_ffn_bg"], (P, EXPERTS))], axis=1)
    pre = np.concatenate([rows_to(wx[:DI]), rows_to(a["L0_attn_W_dt"].T)], axis=1)
    cmod = np.concatenate([a["L0_c"].T, a["L1_c"].T], axis=1)
    wmod = np.concatenate([a["L0_wmod"], a["L1_wmod"]], axis=1)
    arrays = {"in_x": a["L0_attn_x"], "in_wts": wts, "in_vecs": vecs, "in_pre": pre, "in_cmod": cmod, "in_wmod": wmod}
    arrays = {k: np.ascontiguousarray(t) for k, t in arrays.items()}

    nc = bacc.Bacc("TRN2", target_bir_lowering=False, num_devices=1)
    args = [nc.dram_tensor(k, t.shape, mybir.dt.from_np(t.dtype), kind="ExternalInput").ap() for k, t in arrays.items()]
    args.append(nc.dram_tensor("out_0", (BATCH, L, P), F32, kind="ExternalOutput").ap())
    build(nc, *args)
    r = run_bass_kernel_spmd(nc, [arrays], core_ids=[0])
    return r.results[0]["out_0"]
```

```python
from contextlib import ExitStack

import concourse.bass as bass
from concourse import mybir

F32 = mybir.dt.float32
BF16 = mybir.dt.bfloat16
U32 = mybir.dt.uint32
ALU = mybir.AluOpType
ACT = mybir.ActivationFunctionType

P = 128
BATCH, L = 8, 1024
NT = L // P
HALF = 512
TH = HALF // P
DI = 256
ND = DI // P
NS = 16
TAPS = 4
HID = 512
NM = HID // P
EXPERTS, RANK = 8, 64
CHUNK = 16
HEADS = 16
EPS = 1e-5
SPLIT = 3

W_PARTS = [("w_in", 2 * DI), ("w_bc", ND * 2 * NS), ("w_out", ND * P), ("w1", HID), ("w2", HID), ("h1", NM * HID),
           ("h2", NM * HID), ("w3", NM * P), ("b_in", P), ("b_gate", 2 * P), ("b_out", P), ("e1", HID),
           ("e2", NM * P), ("e_gate", EXPERTS)]
W_AT, W_COLS = {}, 0
for _name, _n in W_PARTS:
    W_AT[_name] = W_COLS
    W_COLS += _n
V_PARTS = [("conv_w", ND * TAPS), ("conv_b", ND), ("b_dt", ND), ("a_log", ND * NS), ("d", ND), ("ln_g", 1),
           ("ln_b", 1), ("w1_s", NM), ("w2_s", NM), ("h1_s", NM), ("h2_s", NM), ("w3_s", 1), ("l_g", 1), ("l_b", 1),
           ("gate_b", 2), ("eig", 1), ("bg", EXPERTS)]
V_AT, V_COLS = {}, 0
for _name, _n in V_PARTS:
    V_AT[_name] = V_COLS
    V_COLS += _n
(SA0, CA0, G_LN, G_LB, SB0, CB0, G_FFN, SA1, CA1, G_ATT, SB1, CB1, G_MOE) = range(13)
NVEC = 13


RING = 6
EXPS = 4
TICKS = range(-6, 2 * NS + 1)
Z_TICK = 27
IN_STEPS = 10
SLOTS = [("in", i) for i in range(IN_STEPS)] + [("scan", t) for t in TICKS] + [("out", i) for i in range(2 * ND)]


def norm_stages(n):
    return ([(kind, n, h) for h in range(2) for kind in ("stat", "rstd")]
            + [(kind, n, h) for h in range(2) for kind in ("apply", "turn")])


def rest_stages():
    out = [("rows",)] + [("mix", h) for h in range(2)] + [(kind, 0, h) for h in range(2) for kind in ("stat", "rstd")]
    out += [("apply", 0, 0), ("apply", 0, 1), ("mixed",)] + norm_stages(1)
    for h in range(2):
        out += [(kind, h, m) for kind in ("gated", "hidden1", "hidden2") for m in range(NM)] + [("down", h)]
    out += norm_stages(2) + [("proj", h) for h in range(2)] + norm_stages(3)
    out += [("gates",)] + [("recur", k) for k in range(5)] + [("att_out", h) for h in range(2)] + norm_stages(4)
    out += [("route", k) for k in range(4)]
    out += [("expert", 0, m) for m in range(NM)] + [("expert", 1, 0), ("expert", 1, 1), ("combine", 0)]
    out += [("expert", 1, 2), ("expert", 1, 3), ("combine", 1)]
    return out


PARTS = {"stat": "V", "rstd": "G", "apply": "V", "turn": "ES", "proj": "E", "gates": "ES", "att_out": "EV",
         "expert": "ESV", "combine": "EV", "rows": "EV", "mix": "E", "mixed": "V", "gated": "ESV", "hidden1": "ES",
         "hidden2": "ES", "down": "EV", ("recur", 0): "V", ("recur", 1): "V", ("recur", 2): "S", ("recur", 3): "V",
         ("recur", 4): "V", ("route", 0): "E", ("route", 1): "SV", ("route", 2): "V", ("route", 3): "ES"}

PLACES = {
    "E": [1, 3, 5, 8, 8, 9, 10, 11, 12, 12, 13, 14, 14, 15, 16, 16, 18, 20, 21, 22, 22, 22, 24, 25, 28, 29, 31, 32,
          33, 34, 36, 37, 37, 37, 37, 39, 39, 39, 41, 41, 41, 41, 42, 43, 44, 45, 46, 46, 47, 47, 48, 49, 49, 51],
    "S": [8, 8, 9, 10, 11, 11, 13, 13, 13, 15, 16, 18, 18, 19, 21, 21, 22, 23, 25, 25, 28, 31, 31, 33, 33, 35, 36, 37,
          39, 39, 39, 39, 40, 40, 42, 43, 43, 43, 44, 44, 44, 44, 47, 49],
    "G": [0, 6, 6, 6, 37, 37, 37, 37, 41, 41],
    "V": [1, 5, 6, 7, 7, 7, 7, 7, 7, 8, 11, 11, 13, 13, 21, 22, 22, 23, 24, 37, 37, 37, 37, 37, 38, 38, 38, 38, 40,
          40, 41, 41, 42, 42, 42, 42, 42, 42, 43, 43, 45, 45, 46, 46, 46, 48, 48, 49, 49, 51],
}


def rest_plan(do_rest):
    plan = {(engine, slot): [] for engine in PLACES for slot in SLOTS}
    for engine, places in PLACES.items():
        stages = [stage for stage in rest_stages() if engine in (PARTS[stage] if stage in PARTS else PARTS[stage[0]])]
        for place, stage in zip(places, stages, strict=True):
            if do_rest:
                plan[engine, SLOTS[place]].append(stage)
    return plan


TURNED = {1: 0, 2: 2, 4: 4}
UPDATES = {"down": 1, "att_out": 3, "combine": 5}
ALL_UPDATES = 7


def bank_uses(do_scan, plan):
    uses = []
    for slot in SLOTS:
        if do_scan:
            uses += {
                ("in", 1): [(("in_t", h), "hcm", h + 1) for h in range(2)],
                **{("in", 2 + d): [(("xs", d, h), "xs_sb", 2 * d + h + 1) for h in range(2)] for d in range(ND)},
                ("scan", Z_TICK): [(("z", d, h), "z", 2 * d + h + 1) for d in range(ND) for h in range(2)],
                **{("in", 6 + d): [(("dt", d, h), "abs_dt", 2 * d + h + 1) for h in range(2)] for d in range(ND)},
                ("in", 8): [("bc", "c_sb", 1)],
                ("in", 9): [(("b_t", 0), "b_sb", 1), (("b_t", 1), "b_sb", 2)],
                **{("out", i): [(("y_t", i // 2, i % 2), "y_sum", i + 1)] for i in range(2 * ND)},
            }.get(slot, [])
        for stage in plan["E", slot]:
            kind, *at = stage
            h = at[0] if at else 0
            i = NM * h + at[1] + 1 if len(at) == 2 else 0
            if kind == "turn":
                n, h = at
                uses += [(stage, "xpc", h + 1) if n == 3 else (stage, "hc", TURNED[n] + h + 1)]
            elif kind == "route":
                uses += {0: [("logits", "lg", 1)], 3: [(("g_t", 0), "gs", 1), (("g_t", 1), "gs", 2)]}.get(h, [])
            else:
                uses += {
                    "rows": [("rows0", "wog", 1), ("rows1", "w2g", 1)],
                    "mix": [(stage, "r_norm", 4 * (h + 1))],
                    "gated": [(("gated_a", *at), "gate_a", i), (("gated_b", *at), "h0", i)],
                    "hidden1": [(stage, "g1", i)],
                    "hidden2": [(stage, "g2", i)],
                    "down": [(stage, "x_upd", UPDATES["down"] + h + 1)],
                    "proj": [(stage, "r_norm", 8 * 3 + 4 * (h + 1))],
                    "gates": [((part, x), sem, x + 1) for x in range(2)
                              for part, sem in (("alpha", "tanh_a"), ("beta", "tanh_b"))],
                    "att_out": [(stage, "x_upd", UPDATES["att_out"] + h + 1)],
                    "expert": [(("exp_h", *at), "exp_g", i), (("exp_g", *at), "gx", i)],
                    "combine": [(stage, "x_upd", UPDATES["combine"] + h + 1)],
                }.get(kind, [])
    return uses


def bank_plan(uses):
    return {name: (i % 3, i // 3, *(uses[i - 3][1:] if i >= 3 else (None, 0))) for i, (name, _, _) in enumerate(uses)}


SEMS = """res x_in cur cur_r rest_x_in diag rows w3g wog w2g stored
p_stat p_aggr p_var p_rstd p_norm hcm pad xs_sb conv u z relu_dt abs_dt exp_dt ln_dt delta du bc_split b_sb c_sb
b_full b_spread da dbu h_done ht_full acc y_sum y
r_stat r_aggr r_var r_rstd r_norm on_g x_g2 x_upd hc gate_a h0 g1 g2
tanh_a tanh_b alpha a_shift cp cp_abs b_in bg_in c_in c_last q aq hout xpc xph q0
lg top idx gap tg wts one g_split gs exp_g gx""".split()


def build(nc, x, wts, vecs, pre, cmod, wmod, out):
    with ExitStack() as ctx:
        def sb(name, shape, dt=F32):
            return ctx.enter_context(nc.sbuf_tensor(name, shape, dt))

        def ps(name, shape):
            return ctx.enter_context(nc.psum_tensor(name, shape, F32))

        s = {n: ctx.enter_context(nc.semaphore("s_" + n)) for n in SEMS}
        bank_full = [ctx.enter_context(nc.semaphore(f"bank_full{i}")) for i in range(3)]
        pre_sem = [ctx.enter_context(nc.semaphore(f"pre{i}")) for i in range(7)]
        clear = range(s[SEMS[0]].num, bank_full[-1].num + 1)

        W = sb("W", [P, W_COLS])
        V = sb("V", [P, V_COLS])
        ident = sb("ident", [P, P])
        ones = sb("ones", [P, P])
        mhalf = sb("mhalf", [P, NT])
        iota_e = sb("iota_e", [P, EXPERTS])
        starts = sb("starts", [P, L])
        sel_b = sb("sel_b", [SPLIT * NS, NS, P], BF16)
        sel_g = sb("sel_g", [SPLIT * EXPERTS, EXPERTS, RANK], BF16)
        w_dtx = sb("w_dtx", [P, ND, DI])
        neg_a = sb("neg_a", [P, ND, NS])
        vec = sb("vec", [P, BATCH, NVEC])
        eig_half = sb("eig_half", [P, 1])
        gate_bh = sb("gate_bh", [P, 2])
        small = sb("small", [P, 256])

        cur = sb("cur", [P, NVEC])
        cur_r = sb("cur_r", [P, NVEC])
        stat = sb("stat", [P, NT, 6])
        aggr = sb("aggr", [P, NT, 2])
        rstd = sb("rstd", [P, NT])
        var = sb("var", [P, NT])
        u = sb("u", [P, ND, L])
        hcm = sb("hcm", [P, L])
        delta = sb("delta", [P, ND, L])
        zs = delta
        du = sb("du", [P, ND, L])
        c_tok = sb("c_tok", [P, NT, NS])
        b_tok = sb("b_tok", [P, NT, SPLIT * NS])
        b_hi = sb("b_hi", [P, 2, NT, NS], BF16)
        b_sb = sb("b_sb", [SPLIT * NS, L], BF16)
        b_spread = sb("b_spread", [P, 2, L])
        da = sb("da", [P, RING, L])
        hst = sb("hst", [P, RING, L])
        acc = sb("acc", [P, NT, DI])
        ycm = sb("ycm", [P, ND + 1, L])
        xpad = hst[:, :, :].rearrange("p a b -> p (a b)")[:, 0:2 * (L + 4)].rearrange("p (d t) -> p d t", d=2)
        soft = da[:, 0:2, :]
        xt = da[:, 2, :].rearrange("p (j c) -> p j c", c=P)
        xn = da[:, 3, :].rearrange("p (j c) -> p j c", c=P)

        xq = sb("xq", [P, NT, P])
        xr = sb("xr", [P, NT, P])
        rn = sb("rn", [P, NT, P])
        rstat = sb("rstat", [P, NT, 6])
        raggr = sb("raggr", [P, NT, 2])
        rrstd = sb("rrstd", [P, NT])
        rvar = sb("rvar", [P, NT])
        hc = sb("hc", [P, L])
        rows = sb("rows", [P, 2, P])
        w3g = sb("w3g", [P, NM, P])
        wog = sb("wog", [P, P])
        w2g = sb("w2g", [P, NM, P])
        ga = sb("ga", [P, HALF])
        hid = sb("hid", [P, 4, L])
        h0 = hid[:, 0:2, :].rearrange("p a (m t) -> p (a m) t", t=HALF)
        g1 = hid[:, 2:4, :].rearrange("p a (m t) -> p (a m) t", t=HALF)
        g2 = h0
        weighed = (h0, g1)
        diag = hid[:, 3, 0:5 * P].rearrange("p (i c) -> p i c", c=P)
        rec = sb("rec", [P, L])
        xpc, al, ash, bb = hid[:, 0, :], hid[:, 1, :], hid[:, 2, :], hid[:, 3, :]
        qs = sb("qs", [P, L + 1])
        lg = sb("lg", [P, NT, EXPERTS])
        top = sb("top", [P, NT, 8])
        idx = sb("idx", [P, NT, 8], U32)
        idf = sb("idf", [P, NT, 8])
        gap = sb("gap", [P, NT, 2])
        oh = sb("oh", [P, 2, NT, EXPERTS])
        g_tok = sb("g_tok", [P, NT, SPLIT * EXPERTS])
        g_hi = sb("g_hi", [P, 2, NT, EXPERTS], BF16)
        g_sb = sb("g_sb", [SPLIT * EXPERTS, L], BF16)

        ht = [ps(f"ht{i}", [P, TH, DI]) for i in range(2)]
        bspr = ps("bspr", [P, HALF])
        bank = [ps(f"bank{i}", [P, HALF]) for i in range(3)]

        def w(name, n, at=0):
            return W[:, W_AT[name] + at:W_AT[name] + at + n]

        def v(name, i=0, n=1):
            return V[:, V_AT[name] + i:V_AT[name] + i + n]

        def half(ap, h):
            return ap[:, h * HALF:(h + 1) * HALF]

        ld, pv, pp, pa, pt, px, rest_wts = pre_sem
        wx = da[:, 0:2, :].rearrange("p a b -> p (a b)")[:, 0:2 * ND * DI].rearrange("p (a j k) -> p a j k", a=2, j=ND)
        cm = small[:, 0:2 * BATCH]
        cms = small[:, 16:16 + 2 * BATCH]
        wm = hst[:, 0:2, :].rearrange("p a b -> p (a b)")[:, 0:2 * 6 * P]
        modp = bank[0][:, 0:12 * BATCH].rearrange("p (m b) -> p m b", b=BATCH)
        mod = small[:, 32:32 + 12 * BATCH].rearrange("p (m b) -> p m b", b=BATCH)
        sgn = small[:, 128:128 + 4 * BATCH].rearrange("p (m b) -> p m b", b=BATCH)
        mag = small[:, 160:160 + 4 * BATCH].rearrange("p (m b) -> p m b", b=BATCH)
        s48 = small[0:48, 192:192 + NS]
        s24 = small[0:24, 208:208 + EXPERTS]

        with nc.Block() as block:
            @block.sync
            def _(sp):
                sp.dma_start(cm, cmod).then_inc(ld, 16)
                sp.dma_start(wm, wmod).then_inc(ld, 16)
                sp.dma_start(V[:], vecs).then_inc(ld, 16)
                sp.dma_start(wx.rearrange("p a j k -> p (a j k)"), pre).then_inc(ld, 16)
                sp.dma_start(W[:, 0:W_AT["w_out"]], wts[:, 0:W_AT["w_out"]]).then_inc(ld, 16)
                sp.dma_start(xt, x[0].rearrange("(j p) c -> p j c", p=P)).then_inc(px, 16)
                sp.dma_start(W[:, W_AT["w_out"]:], wts[:, W_AT["w_out"]:]).then_inc(rest_wts, 16)
                sp.wait_ge(ld, 80)
                sp.wait_ge(px, 16)

            @block.gpsimd
            def _(pool):
                nc.gpsimd.memset(ident[:], 0.0).then_inc(pp, 1)
                nc.gpsimd.memset(ones[:], 1.0).then_inc(pp, 1)
                nc.gpsimd.memset(mhalf[:], -0.5).then_inc(pp, 1)
                nc.gpsimd.memset(starts[:], 0.0).then_inc(pp, 1)
                nc.gpsimd.iota(iota_e[:], pattern=[[1, EXPERTS]], base=0, channel_multiplier=0,
                               allow_small_or_imprecise_dtypes=True).then_inc(pp, 1)
                pool.wait_ge(pp, 5)
                nc.gpsimd.affine_select(out=ident[:], in_=ident[:], compare_op=ALU.not_equal, fill=1.0, base=0,
                                        pattern=[[-1, P]], channel_multiplier=1).then_inc(pp, 1)
                nc.gpsimd.memset(starts[:, 0:L:CHUNK], 1.0).then_inc(pp, 1)

            @block.scalar
            def _(act):
                act.wait_ge(ld, 80)
                nc.scalar.activation(cms, cm, ACT.Silu).then_inc(pa, 1)
                nc.scalar.activation(neg_a[:].rearrange("p a b -> p (a b)"), v("a_log", 0, ND * NS),
                                     ACT.Exp).then_inc(pa, 1)
                nc.scalar.activation(eig_half[:], v("eig"), ACT.Tanh).then_inc(pa, 1)

            @block.tensor
            def _(pe):
                pe.wait_ge(pa, 1)
                for m in range(12):
                    last = nc.tensor.matmul(modp[:, m, :], wm[:, m * P:(m + 1) * P],
                                            cms[:, (m // 6) * BATCH:(m // 6 + 1) * BATCH], start=True, stop=True)
                last.then_inc(pt, 1)
                for k in range(ND):
                    for j in range(ND):
                        last = nc.tensor.matmul(bank[1][:, k * DI:(k + 1) * DI], wx[:, 0, j, k * P:(k + 1) * P],
                                                wx[:, 1, j, :], start=(j == 0), stop=(j == ND - 1))
                last.then_inc(pt, 1)

            @block.vector
            def _(dve):
                steps = [0]

                def link(ins):
                    steps[0] += 1
                    ins.then_inc(pv, 1)
                    dve.wait_ge(pv, steps[0])

                dve.wait_ge(pp, 7)
                link(nc.vector.tensor_tensor(s48, ident[0:48, 0:16], ident[0:48, 16:32], ALU.add))
                link(nc.vector.tensor_tensor(s48, s48, ident[0:48, 32:48], ALU.add))
                link(nc.vector.tensor_copy(sel_b[:], s48[:, :, None].to_broadcast([48, NS, P])))
                link(nc.vector.tensor_tensor(s24, ident[0:24, 0:8], ident[0:24, 8:16], ALU.add))
                link(nc.vector.tensor_tensor(s24, s24, ident[0:24, 16:24], ALU.add))
                link(nc.vector.tensor_copy(sel_g[:], s24[:, :, None].to_broadcast([24, EXPERTS, RANK])))
                dve.wait_ge(pa, 3)
                link(nc.vector.tensor_scalar(neg_a[:], neg_a[:], -1.0, None, ALU.mult))
                link(nc.vector.tensor_scalar(eig_half[:], eig_half[:], 0.5, None, ALU.mult))
                link(nc.vector.tensor_scalar(gate_bh[:], v("gate_b", 0, 2), 0.5, None, ALU.mult))
                dve.wait_ge(pt, 2)
                link(nc.vector.tensor_copy(w_dtx[:].rearrange("p a b -> p (a b)"), bank[1][:]))
                link(nc.vector.tensor_copy(mod, modp))
                gates = mod[:, 2:12:3, :]
                link(nc.vector.tensor_scalar(sgn, gates, 0.0, 2.0, ALU.is_ge, ALU.mult))
                link(nc.vector.tensor_scalar(mag, gates, -1.0, None, ALU.mult))
                link(nc.vector.tensor_tensor(mag, mag, gates, ALU.max))
                link(nc.vector.tensor_scalar(mag, mag, 0.25, None, ALU.max))
                link(nc.vector.scalar_tensor_tensor(out=mag, in0=sgn, scalar=-1.0, in1=mag, op0=ALU.add,
                                                    op1=ALU.mult))
                for i, m in ((SA0, 0), (SB0, 3), (SA1, 6), (SB1, 9)):
                    link(nc.vector.tensor_copy(vec[:, :, i], mod[:, m, :]))
                for i, m in ((CA0, 1), (CB0, 4), (CA1, 7), (CB1, 10)):
                    link(nc.vector.tensor_scalar(vec[:, :, i], mod[:, m, :], 1.0, None, ALU.add))
                for i, g, col in ((G_LN, 0, v("ln_g")), (G_LB, 0, v("ln_b")), (G_FFN, 1, v("w3_s"))):
                    link(nc.vector.tensor_scalar(vec[:, :, i], mag[:, g, :], col, None, ALU.mult))
                link(nc.vector.tensor_scalar(vec[:, :, G_ATT], mag[:, 2, :], 0.5, None, ALU.mult))
                link(nc.vector.tensor_scalar(vec[:, :, G_MOE], mag[:, 3, :], 2.0, None, ALU.mult))

        def body(do_scan, do_rest, load_next, b):
            plan = rest_plan(do_rest)
            banks = bank_plan(bank_uses(do_scan, plan))
        
            def full(eng, name):
                k, n, _, _ = banks[name]
                eng.wait_ge(bank_full[k], n + 1)
                return bank[k]

            def take(pe, name):
                k, _, reader, count = banks[name]
                if reader:
                    pe.wait_ge(s[reader], count)
                return bank[k]

            def filled(ins, name):
                ins.then_inc(bank_full[banks[name][0]], 1)

            with nc.Block() as block:
                @block.sync
                def _(sp):
                    if not do_rest:
                        sp.wait_ge(rest_wts, 16)
                    if do_rest:
                        sp.dma_start(xq[:], x[bass.ds(b - 1, 1)].rearrange("o (j p) c -> p (o j) c", p=P)).then_inc(
                            s["rest_x_in"], 16)
                    if load_next:
                        sp.wait_ge(s["h_done"], 2 * NS)
                        sp.dma_start(xt, x[bass.ds(b + 1, 1)].rearrange("o (j p) c -> p (o j) c", p=P)).then_inc(
                            s["x_in"], 16)
                        sp.wait_ge(s["x_in"], 16)
                    if do_rest:
                        sp.wait_ge(s["x_upd"], ALL_UPDATES)
                        sp.dma_start(out[bass.ds(b - 1, 1)].rearrange("o (j p) c -> p (o j) c", p=P), xr[:]).then_inc(
                            s["stored"], 16)
                        sp.wait_ge(s["stored"], 16)

                @block.tensor
                def _(pe):
                    def turn(name, src, sem, count):
                        pe.wait_ge(sem, count)
                        o = take(pe, name)
                        for jj in range(TH):
                            last = nc.tensor.transpose(o[:, jj * P:(jj + 1) * P], src(jj), ident[:])
                        filled(last, name)

                    def project(part, at, d, h):
                        o = take(pe, (part, d, h))
                        filled(nc.tensor.matmul(o[:], w("w_in", P, at + d * P), half(hcm[:], h), start=True,
                                                stop=True), (part, d, h))

                    def mixer_in(k):
                        if k == 1:
                            for h in range(2):
                                turn(("in_t", h), lambda jj: xn[:, h * TH + jj, :], s["p_norm"], 4 * (h + 1))
                        elif k in (2, 3):
                            pe.wait_ge(s["hcm"], 2)
                            for h in range(2):
                                project("xs", 0, k - 2, h)
                        elif k in (6, 7):
                            m = k - 6
                            pe.wait_ge(s["u"], 2)
                            for h in range(2):
                                o = take(pe, ("dt", m, h))
                                for i in range(ND):
                                    last = nc.tensor.matmul(o[:], w_dtx[:, i, m * P:(m + 1) * P],
                                                            half(u[:, i, :], h), start=(i == 0), stop=(i == ND - 1))
                                filled(last, ("dt", m, h))
                        elif k == 8:
                            o = take(pe, "bc")
                            for j in range(NT):
                                for i in range(ND):
                                    last = nc.tensor.matmul(o[:, j * 2 * NS:(j + 1) * 2 * NS],
                                                            u[:, i, j * P:(j + 1) * P],
                                                            w("w_bc", 2 * NS, i * 2 * NS), start=(i == 0),
                                                            stop=(i == ND - 1))
                            filled(last, "bc")
                        elif k == 9:
                            pe.wait_ge(s["bc_split"], 5)
                            for h in range(2):
                                o = take(pe, ("b_t", h))
                                for jj in range(TH):
                                    last = nc.tensor.transpose(o[0:SPLIT * NS, jj * P:(jj + 1) * P],
                                                               b_tok[:, h * TH + jj, :], ident[:])
                                filled(last, ("b_t", h))

                    def scan(t):
                        n, c = t // 2, t % 2
                        if n + 3 < NS:
                            i = 2 * (n + 3) + c
                            if i == 0:
                                pe.wait_ge(s["b_sb"], 2)
                            else:
                                pe.wait_ge(s["b_spread"], i)
                            nc.tensor.matmul(bspr[:], sel_b[:, n + 3, :], half(b_sb[:], c), start=True,
                                             stop=True).then_inc(s["b_full"], 1)
                        if 0 <= n < NS:
                            pe.wait_ge(s["h_done"], 2 * n + 2)
                            if n >= 1:
                                pe.wait_ge(s["acc"], TH * (2 * n - 1 + c))
                            for jj in range(TH):
                                for d in range(ND):
                                    at = (c * TH + jj) * P
                                    last = nc.tensor.transpose(ht[c][:, jj, d * P:(d + 1) * P],
                                                               hst[:, (2 * n + d) % RING, at:at + P], ident[:])
                            last.then_inc(s["ht_full"], 1)
                        if t == Z_TICK:
                            for d in range(ND):
                                for h in range(2):
                                    project("z", DI, d, h)

                    def rest(stage):
                        kind = stage[0]
                        if kind == "rows":
                            pe.wait_ge(s["diag"], 5)
                            for name, a, n in (("rows0", 0, 4), ("rows1", 4, 1)):
                                o = take(pe, name)
                                for i in range(n):
                                    last = nc.tensor.matmul(o[:, i * P:(i + 1) * P], ones[:], diag[:, a + i, :],
                                                            start=True, stop=True)
                                filled(last, name)
                        elif kind == "mix":
                            h = stage[1]
                            o = take(pe, stage)
                            for jj in range(TH):
                                t = (h * TH + jj) * P
                                for k in range(ND + 1):
                                    rhs = w("w_out", P, k * P) if k < ND else ident[:]
                                    last = nc.tensor.matmul(o[:, jj * P:(jj + 1) * P], ycm[:, k, t:t + P], rhs,
                                                            start=(k == 0), stop=(k == ND))
                            filled(last, stage)
                        elif kind == "turn":
                            n, h = stage[1:]
                            turn(stage, lambda jj: rn[:, h * TH + jj, :], s["r_norm"],
                                 8 * n + 4 * (h + 1))
                        elif kind == "gated":
                            h, m = stage[1:]
                            pe.wait_ge(s["hc"], TURNED[1] + 1 + h)
                            for part, wt in (("gated_a", "w1"), ("gated_b", "w2")):
                                o = take(pe, (part, h, m))
                                filled(nc.tensor.matmul(o[:], w(wt, P, m * P), half(hc[:], h), start=True, stop=True),
                                       (part, h, m))
                        elif kind in ("hidden1", "hidden2"):
                            h, m = stage[1:]
                            wt, src, sem = ("h1", h0, s["h0"]) if kind == "hidden1" else ("h2", g1, s["g1"])
                            o = take(pe, stage)
                            for k in range(NM):
                                if m == 0:
                                    pe.wait_ge(sem, NM * h + k + 1)
                                last = nc.tensor.matmul(o[:], w(wt, P, k * HID + m * P), src[:, k, :], start=(k == 0),
                                                        stop=(k == NM - 1))
                            filled(last, stage)
                        elif kind == "down":
                            h = stage[1]
                            pe.wait_ge(s["g2"], NM * (h + 1))
                            pe.wait_ge(s["w3g"], 1)
                            o = take(pe, stage)
                            for jj in range(TH):
                                for k in range(NM):
                                    last = nc.tensor.matmul(o[:, jj * P:(jj + 1) * P], g2[:, k, jj * P:(jj + 1) * P],
                                                            w3g[:, k, :], start=(k == 0), stop=(k == NM - 1))
                            filled(last, stage)
                        elif kind == "proj":
                            h = stage[1]
                            pe.wait_ge(s["hc"], TURNED[2] + 1 + h)
                            o = take(pe, stage)
                            for jj in range(TH):
                                t = (h * TH + jj) * P
                                last = nc.tensor.matmul(o[:, jj * P:(jj + 1) * P], hc[:, t:t + P], w("b_in", P),
                                                        start=True, stop=True)
                            filled(last, stage)
                        elif kind == "gates":
                            pe.wait_ge(s["xpc"], 2)
                            for h in range(2):
                                for i, part in enumerate(("alpha", "beta")):
                                    o = take(pe, (part, h))
                                    filled(nc.tensor.matmul(o[:], w("b_gate", P, i * P), half(xpc, h), start=True,
                                                            stop=True), (part, h))
                        elif kind == "att_out":
                            pe.wait_ge(s["hout"], 1)
                            h = stage[1]
                            o = take(pe, stage)
                            for jj in range(TH):
                                t = (h * TH + jj) * P
                                last = nc.tensor.matmul(o[:, jj * P:(jj + 1) * P], rec[:, t:t + P], wog[:],
                                                        start=True, stop=True)
                            filled(last, stage)
                        elif stage == ("route", 0):
                            pe.wait_ge(s["hc"], TURNED[4] + 2)
                            o = take(pe, "logits")
                            for j in range(NT):
                                last = nc.tensor.matmul(o[:, j * EXPERTS:(j + 1) * EXPERTS], hc[:, j * P:(j + 1) * P],
                                                        w("e_gate", EXPERTS), start=True, stop=True)
                            filled(last, "logits")
                        elif stage == ("route", 3):
                            pe.wait_ge(s["g_split"], 5)
                            for h in range(2):
                                o = take(pe, ("g_t", h))
                                for jj in range(TH):
                                    last = nc.tensor.transpose(o[0:SPLIT * EXPERTS, jj * P:(jj + 1) * P],
                                                               g_tok[:, h * TH + jj, :], ident[:])
                                filled(last, ("g_t", h))
                        elif kind == "expert":
                            h, m = stage[1:]
                            pe.wait_ge(s["gs"], 2)
                            o = take(pe, ("exp_h", h, m))
                            filled(nc.tensor.matmul(o[:], w("e1", P, m * P), half(hc[:], h), start=True, stop=True),
                                   ("exp_h", h, m))
                            o = take(pe, ("exp_g", h, m))
                            filled(nc.tensor.matmul(o[:], sel_g[:, 2 * m:2 * m + 2, :].rearrange("p a b -> p (a b)"),
                                                    half(g_sb[:], h), start=True, stop=True), ("exp_g", h, m))
                        elif kind == "combine":
                            h = stage[1]
                            pe.wait_ge(s["gx"], NM * (h + 1))
                            o = take(pe, stage)
                            for jj in range(TH):
                                for k in range(NM):
                                    last = nc.tensor.matmul(o[:, jj * P:(jj + 1) * P],
                                                            weighed[h][:, k, jj * P:(jj + 1) * P], w2g[:, k, :],
                                                            start=(k == 0), stop=(k == NM - 1))
                            filled(last, stage)

                    def mixer_end(d, h):
                        pe.wait_ge(s["acc"], NT * NS)
                        o = take(pe, ("y_t", d, h))
                        for jj in range(TH):
                            last = nc.tensor.transpose(o[:, jj * P:(jj + 1) * P],
                                                       acc[:, h * TH + jj, d * P:(d + 1) * P], ident[:])
                        filled(last, ("y_t", d, h))

                    for slot, k in SLOTS:
                        if do_scan:
                            if slot == "in":
                                mixer_in(k)
                            elif slot == "scan":
                                scan(k)
                            else:
                                mixer_end(k // 2, k % 2)
                        for stage in plan["E", (slot, k)]:
                            rest(stage)

                @block.scalar
                def _(act):
                    def mixer_in(k):
                        if k == 1:
                            act.wait_ge(s["cur"], 1)
                            for h in range(2):
                                o = full(act, ("in_t", h))
                                nc.scalar.activation(half(hcm[:], h), o[:], ACT.Identity,
                                                     bias=cur[:, SA0:SA0 + 1],
                                                     scale=cur[:, CA0:CA0 + 1]).then_inc(s["hcm"], 1)
                        elif k in (2, 3):
                            d = k - 2
                            for h in range(2):
                                o = full(act, ("xs", d, h))
                                at = TAPS - 1 + h * HALF
                                nc.scalar.activation(xpad[:, d, at:at + HALF], o[:], ACT.Copy).then_inc(s["xs_sb"], 1)
                        elif k in (4, 5):
                            d = k - 4
                            act.wait_ge(s["conv"], TAPS * (d + 1))
                            nc.scalar.activation(u[:, d, :], u[:, d, :], ACT.Silu,
                                                 bias=v("conv_b", d)).then_inc(s["u"], 1)
                        if k in (6, 7):
                            d = k - 6
                            for h in range(2):
                                o = full(act, ("dt", d, h))
                                nc.scalar.activation(half(delta[:, d, :], h), o[:], ACT.Relu,
                                                     bias=v("b_dt", d)).then_inc(s["relu_dt"], 1)
                                nc.scalar.activation(half(soft[:, d, :], h), o[:], ACT.Abs,
                                                     bias=v("b_dt", d)).then_inc(s["abs_dt"], 1)
                        elif k == 8:
                            act.wait_ge(s["abs_dt"], 4)
                            nc.scalar.activation(soft, soft, ACT.Exp, scale=-1.0).then_inc(s["exp_dt"], 1)
                            act.wait_ge(s["exp_dt"], 1)
                            nc.scalar.activation(soft, soft, ACT.Ln, bias=1.0).then_inc(s["ln_dt"], 1)
                        elif k == 9:
                            for h in range(2):
                                o = full(act, ("b_t", h))
                                nc.scalar.activation(half(b_sb[:], h), o[0:SPLIT * NS, :], ACT.Copy).then_inc(
                                    s["b_sb"], 1)

                    def scan(t):
                        n, c = t // 2, t % 2
                        if n + 3 < NS:
                            m = n + 3
                            act.wait_ge(s["b_full"], 2 * m + c + 1)
                            if m >= 2:
                                act.wait_ge(s["dbu"], 2 * m - 2)
                            nc.scalar.activation(half(b_spread[:, m % 2, :], c), bspr[:], ACT.Copy).then_inc(
                                s["b_spread"], 1)
                        if t % EXPS == 0:
                            for i in range(t + 4, min(t + 4 + EXPS, 2 * NS)):
                                act.wait_ge(s["delta"], 2)
                                if i >= RING:
                                    act.wait_ge(s["h_done"], i - RING + 1)
                                nc.scalar.activation(da[:, i % RING, :], delta[:, i % 2, :], ACT.Exp,
                                                     scale=neg_a[:, i % 2, i // 2:i // 2 + 1]).then_inc(s["da"], 1)
                        if t == Z_TICK:
                            act.wait_ge(s["da"], 2 * NS)
                            for d in range(ND):
                                for h in range(2):
                                    o = full(act, ("z", d, h))
                                    nc.scalar.activation(half(zs[:, d, :], h), o[:], ACT.Silu).then_inc(s["z"], 1)

                    def mixer_end(d, h):
                        pass

                    def rest(stage):
                        kind = stage[0]
                        if kind == "turn":
                            n, h = stage[1:]
                            o = full(act, stage)
                            if n == 3:
                                nc.scalar.activation(half(xpc, h), o[:], ACT.Identity, bias=v("l_b"),
                                                     scale=v("l_g")).then_inc(s["xpc"], 1)
                            else:
                                bias, scale = {1: (SB0, CB0), 2: (SA1, CA1), 4: (SB1, CB1)}[n]
                                nc.scalar.activation(half(hc[:], h), o[:], ACT.Identity, bias=cur_r[:, bias:bias + 1],
                                                     scale=cur_r[:, scale:scale + 1]).then_inc(s["hc"], 1)
                        elif kind == "gated":
                            h, m = stage[1:]
                            o = full(act, ("gated_a", h, m))
                            if NM * h + m:
                                act.wait_ge(s["h0"], NM * h + m)
                            nc.scalar.activation(ga[:], o[:], ACT.Silu, scale=v("w1_s", m)).then_inc(s["gate_a"], 1)
                        elif kind in ("hidden1", "hidden2"):
                            h, m = stage[1:]
                            dst, col, sem = (g1, "h1_s", s["g1"]) if kind == "hidden1" else (g2, "h2_s", s["g2"])
                            o = full(act, stage)
                            nc.scalar.activation(dst[:, m, :], o[:], ACT.Gelu, scale=v(col, m)).then_inc(sem, 1)
                        elif kind == "gates":
                            for h in range(2):
                                for i, (part, dst, sem) in enumerate((("alpha", al, s["tanh_a"]), ("beta", bb, s["tanh_b"]))):
                                    o = full(act, (part, h))
                                    nc.scalar.activation(half(dst, h), o[:], ACT.Tanh, bias=gate_bh[:, i:i + 1],
                                                               scale=0.5).then_inc(sem, 1)
                        elif stage == ("recur", 2):
                            act.wait_ge(s["cp"], 1)
                            nc.scalar.activation(rec[:], rec[:], ACT.Abs).then_inc(s["cp_abs"], 1)
                        elif stage == ("route", 1):
                            act.wait_ge(s["gap"], 1)
                            nc.scalar.activation(gap[:, :, 0:1], gap[:, :, 0:1], ACT.Tanh, scale=0.5).then_inc(s["tg"], 1)
                        elif stage == ("route", 3):
                            for h in range(2):
                                o = full(act, ("g_t", h))
                                nc.scalar.activation(half(g_sb[:], h), o[0:SPLIT * EXPERTS, :], ACT.Copy).then_inc(s["gs"], 1)
                        elif kind == "expert":
                            h, m = stage[1:]
                            o = full(act, ("exp_h", h, m))
                            nc.scalar.activation(weighed[h][:, m, :], o[:], ACT.Gelu).then_inc(s["exp_g"], 1)

                    for slot, k in SLOTS:
                        if do_scan:
                            if slot == "in":
                                mixer_in(k)
                            elif slot == "scan":
                                scan(k)
                            else:
                                mixer_end(k // 2, k % 2)
                        for stage in plan["S", (slot, k)]:
                            rest(stage)

                @block.gpsimd
                def _(pool):
                    def inv_std(n, h, ag, vr, rs, s_ag, s_vr, s_rs):
                        j = slice(h * TH, (h + 1) * TH)
                        pool.wait_ge(s_ag, 8 * n + 4 * (h + 1))
                        nc.gpsimd.tensor_scalar(vr[:, j], ag[:, j, 1], EPS, None, ALU.add).then_inc(s_vr, 1)
                        pool.wait_ge(s_vr, 2 * n + h + 1)
                        nc.gpsimd.tensor_tensor(rs[:, j], vr[:, j], mhalf[:, j], ALU.pow).then_inc(s_rs, 1)

                    def mixer_in(k):
                        if k == 0:
                            for h in range(2):
                                inv_std(0, h, aggr, var, rstd, s["p_aggr"], s["p_var"], s["p_rstd"])
                        elif k == 9:
                            for d in range(ND):
                                pool.wait_ge(s["delta"], d + 1)
                                nc.gpsimd.tensor_tensor(du[:, d, :], delta[:, d, :], u[:, d, :], ALU.mult).then_inc(
                                    s["du"], 1)
                            pool.wait_ge(s["du"], 2)

                    def scan(t):
                        n, c = t // 2, t % 2
                        if 0 <= n + 2 < NS:
                            i = 2 * (n + 2) + c
                            pool.wait_ge(s["b_spread"], 2 * (n + 2) + 2)
                            if i >= RING:
                                pool.wait_ge(s["ht_full"], 2 * ((i - RING) // 2) + 2)
                            nc.gpsimd.tensor_tensor(hst[:, i % RING, :], du[:, c, :], b_spread[:, (n + 2) % 2, :],
                                                    ALU.mult).then_inc(s["dbu"], 1)

                    def mixer_end(d, h):
                        if (d, h) == (0, 0):
                            if do_rest:
                                full(pool, ("mix", 1))
                            nc.gpsimd.tensor_copy(ycm[:, ND, :], hcm[:]).then_inc(s["res"], 1)

                    def rest(stage):
                        if stage[0] == "rstd":
                            n, h = stage[1:]
                            inv_std(n, h, raggr, rvar, rrstd, s["r_aggr"], s["r_var"], s["r_rstd"])

                    for slot, k in SLOTS:
                        if do_scan:
                            if slot == "in":
                                mixer_in(k)
                            elif slot == "scan":
                                scan(k)
                            else:
                                mixer_end(k // 2, k % 2)
                        for stage in plan["G", (slot, k)]:
                            rest(stage)

                @block.vector
                def _(dve):
                    def statistics(n, h, src, st, ag, s_st, s_ag):
                        for jj in range(TH):
                            nc.vector.bn_stats(st[:, h * TH + jj, :], src(jj)).then_inc(s_st, 1)
                        dve.wait_ge(s_st, 8 * n + 4 * (h + 1))
                        for jj in range(TH):
                            nc.vector.bn_aggr(ag[:, h * TH + jj, :], st[:, h * TH + jj, :]).then_inc(s_ag, 1)

                    def normalize(n, h, src, ag, rs, dst, s_ag, s_rs, s_nm):
                        dve.wait_ge(s_ag, 8 * n + 4 * (h + 1))
                        dve.wait_ge(s_rs, 2 * n + h + 1)
                        for jj in range(TH):
                            j = h * TH + jj
                            nc.vector.tensor_scalar(dst[:, j, :], src(jj), ag[:, j, 0:1], rs[:, j:j + 1], ALU.subtract,
                                                    ALU.mult).then_inc(s_nm, 1)

                    def norm_source(n, h):
                        if n in (0, 3):
                            o = full(dve, ("mix" if n == 0 else "proj", h))
                            return lambda jj: o[:, jj * P:(jj + 1) * P]
                        return lambda jj: xr[:, h * TH + jj, :]

                    def add_half(name, h, count):
                        o = full(dve, name)
                        if count:
                            dve.wait_ge(s["x_upd"], count)
                        xh = xr[:, h * TH:(h + 1) * TH, :].rearrange("p j c -> p (j c)")
                        nc.vector.tensor_tensor(xh, o[:], xh, ALU.add).then_inc(s["x_upd"], 1)

                    def rows_out():
                        nc.vector.tensor_copy(cur_r[:], vec[:, bass.ds(b - 1, 1), :].rearrange("p o n -> p (o n)")
                                              ).then_inc(s["cur_r"], 1)
                        dve.wait_ge(s["cur_r"], 1)
                        for i, col in enumerate((G_LN, G_LB, G_FFN, G_ATT, G_MOE)):
                            nc.vector.tensor_scalar(diag[:, i, :], ident[:], cur_r[:, col:col + 1], None,
                                                    ALU.mult).then_inc(s["diag"], 1)
                        o = full(dve, "rows0")
                        nc.vector.tensor_copy(rows[:].rearrange("p a c -> p (a c)"), o[:, 0:2 * P]).then_inc(
                            s["rows"], 1)
                        nc.vector.tensor_tensor(w3g[:], w("w3", NM * P).rearrange("p (k c) -> p k c", k=NM),
                                                o[:, None, 2 * P:3 * P].to_broadcast([P, NM, P]), ALU.mult
                                                ).then_inc(s["w3g"], 1)
                        nc.vector.tensor_tensor(wog[:], w("b_out", P), o[:, 3 * P:4 * P], ALU.mult).then_inc(
                            s["wog"], 1)
                        o = full(dve, "rows1")
                        nc.vector.tensor_tensor(w2g[:], w("e2", NM * P).rearrange("p (k c) -> p k c", k=NM),
                                                o[:, None, 0:P].to_broadcast([P, NM, P]), ALU.mult).then_inc(
                            s["w2g"], 1)

                    def mixed():
                        dve.wait_ge(s["rest_x_in"], 16)
                        dve.wait_ge(s["rows"], 1)
                        nc.vector.tensor_tensor(xr[:], xq[:], rows[:, None, 1, :].to_broadcast([P, NT, P]),
                                                ALU.add).then_inc(s["x_g2"], 1)
                        dve.wait_ge(s["r_norm"], 8)
                        nc.vector.tensor_tensor(rn[:], rn[:], rows[:, None, 0, :].to_broadcast([P, NT, P]),
                                                ALU.mult).then_inc(s["on_g"], 1)
                        dve.wait_ge(s["on_g"], 1)
                        dve.wait_ge(s["x_g2"], 1)
                        nc.vector.tensor_tensor(xr[:], xr[:], rn[:], ALU.add).then_inc(s["x_upd"], 1)

                    def split(dst, hi, n, parts, sem):
                        for i in range(parts - 1):
                            a, c = dst[:, :, i * n:(i + 1) * n], dst[:, :, (i + 1) * n:(i + 2) * n]
                            dve.wait_ge(sem, 2 * i + 1)
                            nc.vector.tensor_copy(hi[:, i, :, :], a).then_inc(sem, 1)
                            dve.wait_ge(sem, 2 * i + 2)
                            nc.vector.tensor_tensor(c, a, hi[:, i, :, :], ALU.subtract).then_inc(sem, 1)

                    def mixer_in(k):
                        if k == 0:
                            nc.vector.tensor_copy(cur[:], vec[:, bass.ds(b, 1), :].rearrange("p o n -> p (o n)")
                                                  ).then_inc(s["cur"], 1)
                            nc.vector.memset(xpad[:, :, 0:TAPS - 1], 0.0).then_inc(s["pad"], 1)
                            for h in range(2):
                                statistics(0, h, lambda jj: xt[:, h * TH + jj, :], stat, aggr, s["p_stat"], s["p_aggr"])
                        elif k == 1:
                            for h in range(2):
                                normalize(0, h, lambda jj: xt[:, h * TH + jj, :], aggr, rstd, xn, s["p_aggr"],
                                          s["p_rstd"], s["p_norm"])
                        elif k in (3, 4):
                            d = k - 3
                            dve.wait_ge(s["pad"], 1)
                            dve.wait_ge(s["xs_sb"], 2 * (d + 1))
                            for i in range(TAPS):
                                tap = v("conv_w", d * TAPS + i)
                                if i == 0:
                                    ins = nc.vector.tensor_scalar(u[:, d, :], xpad[:, d, 0:L], tap, None, ALU.mult)
                                else:
                                    dve.wait_ge(s["conv"], TAPS * d + i)
                                    ins = nc.vector.scalar_tensor_tensor(out=u[:, d, :], in0=xpad[:, d, i:i + L],
                                                                         scalar=tap, in1=u[:, d, :], op0=ALU.mult,
                                                                         op1=ALU.add)
                                ins.then_inc(s["conv"], 1)
                        elif k == 8:
                            o = full(dve, "bc")[:, 0:NT * 2 * NS].rearrange("p (j n) -> p j n", n=2 * NS)
                            nc.vector.tensor_copy(b_tok[:, :, 0:NS], o[:, :, 0:NS]).then_inc(s["bc_split"], 1)
                            nc.vector.tensor_copy(c_tok[:], o[:, :, NS:2 * NS]).then_inc(s["c_sb"], 1)
                            split(b_tok, b_hi, NS, SPLIT, s["bc_split"])
                        elif k == 9:
                            dve.wait_ge(s["ln_dt"], 1)
                            for d in range(ND):
                                nc.vector.tensor_tensor(delta[:, d, :], delta[:, d, :], soft[:, d, :],
                                                        ALU.add).then_inc(s["delta"], 1)

                    def scan(t):
                        n, c = t // 2, t % 2
                        if 0 <= n + 1 < NS:
                            i = 2 * (n + 1) + c
                            dve.wait_ge(s["da"], i + 1)
                            dve.wait_ge(s["dbu"], i + 1)
                            nc.vector.tensor_tensor_scan(hst[:, i % RING, :], da[:, i % RING, :], hst[:, i % RING, :],
                                                         0.0, ALU.mult, ALU.add).then_inc(s["h_done"], 1)
                        if t >= 1:
                            n, c = (t - 1) // 2, (t - 1) % 2
                            dve.wait_ge(s["ht_full"], t)
                            if n == 0:
                                dve.wait_ge(s["c_sb"], 1)
                            else:
                                dve.wait_ge(s["acc"], TH * (2 * n - 1 + c))
                            for jj in range(TH):
                                j = c * TH + jj
                                if n == 0:
                                    ins = nc.vector.tensor_scalar(acc[:, j, :], ht[c][:, jj, :], c_tok[:, j, 0:1], None,
                                                                  ALU.mult)
                                else:
                                    ins = nc.vector.scalar_tensor_tensor(out=acc[:, j, :], in0=ht[c][:, jj, :],
                                                                         scalar=c_tok[:, j, n:n + 1], in1=acc[:, j, :],
                                                                         op0=ALU.mult, op1=ALU.add)
                                ins.then_inc(s["acc"], 1)

                    def rest(stage):
                        kind = stage[0]
                        if kind == "rows":
                            rows_out()
                        elif kind == "mixed":
                            mixed()
                        elif kind == "stat":
                            n, h = stage[1:]
                            before = {1: 1, 2: UPDATES["down"] + 1 + h, 4: UPDATES["att_out"] + 1 + h}
                            if n in before:
                                dve.wait_ge(s["x_upd"], before[n])
                            statistics(n, h, norm_source(n, h), rstat, raggr, s["r_stat"], s["r_aggr"])
                        elif kind == "apply":
                            n, h = stage[1:]
                            normalize(n, h, norm_source(n, h), raggr, rrstd, rn, s["r_aggr"], s["r_rstd"], s["r_norm"])
                        elif kind == "gated":
                            h, m = stage[1:]
                            o = full(dve, ("gated_b", h, m))
                            dve.wait_ge(s["gate_a"], NM * h + m + 1)
                            nc.vector.scalar_tensor_tensor(out=h0[:, m, :], in0=o[:], scalar=v("w2_s", m), in1=ga[:],
                                                           op0=ALU.mult, op1=ALU.mult).then_inc(s["h0"], 1)
                        elif kind in ("down", "att_out", "combine"):
                            add_half(stage, stage[1], stage[1] + UPDATES[kind])
                        elif stage == ("recur", 0):
                            dve.wait_ge(s["tanh_a"], 2)
                            nc.vector.tensor_scalar(al, al, eig_half[:], eig_half[:], ALU.mult,
                                                    ALU.add).then_inc(s["alpha"], 1)
                            dve.wait_ge(s["alpha"], 1)
                            nc.vector.tensor_copy(ash[:, 1:L], al[:, 0:L - 1]).then_inc(s["a_shift"], 1)
                            dve.wait_ge(s["a_shift"], 1)
                            nc.vector.memset(ash[:, 0:L:CHUNK], 0.0).then_inc(s["a_shift"], 1)
                        elif stage == ("recur", 1):
                            dve.wait_ge(s["tanh_b"], 2)
                            nc.vector.scalar_tensor_tensor(out=bb, in0=bb, scalar=1.0, in1=xpc, op0=ALU.add,
                                                           op1=ALU.mult).then_inc(s["b_in"], 1)
                            dve.wait_ge(s["a_shift"], 2)
                            nc.vector.tensor_tensor_scan(rec[:], ash, starts[:], 0.0, ALU.mult,
                                                         ALU.add).then_inc(s["cp"], 1)
                        elif stage == ("recur", 3):
                            dve.wait_ge(s["cp_abs"], 1)
                            dve.wait_ge(s["b_in"], 1)
                            nc.vector.scalar_tensor_tensor(out=rec[:], in0=rec[:], scalar=1e-8, in1=bb, op0=ALU.is_gt,
                                                           op1=ALU.mult).then_inc(s["bg_in"], 1)
                            dve.wait_ge(s["bg_in"], 1)
                            nc.vector.tensor_tensor(rec[:], rec[:], al, ALU.mult).then_inc(s["c_in"], 1)
                            dve.wait_ge(s["c_in"], 1)
                            nc.vector.tensor_copy(rec[:, CHUNK - 1:L:CHUNK], bb[:, CHUNK - 1:L:CHUNK]).then_inc(s["c_last"], 1)
                        elif stage == ("recur", 4):
                            nc.vector.memset(qs[:, 0:1], 0.0).then_inc(s["q0"], 1)
                            dve.wait_ge(s["c_last"], 1)
                            nc.vector.tensor_tensor_scan(qs[:, 1:L + 1], al, rec[:], 0.0, ALU.mult,
                                                         ALU.add).then_inc(s["q"], 1)
                            dve.wait_ge(s["q"], 1)
                            dve.wait_ge(s["q0"], 1)
                            nc.vector.tensor_tensor(rec[:], al, qs[:, 0:L], ALU.mult).then_inc(s["aq"], 1)
                            dve.wait_ge(s["aq"], 1)
                            nc.vector.tensor_tensor(rec[:], rec[:], bb, ALU.add).then_inc(s["hout"], 1)
                        elif stage == ("route", 1):
                            o = full(dve, "logits")[:, 0:NT * EXPERTS].rearrange("p (j e) -> p j e", e=EXPERTS)
                            nc.vector.tensor_tensor(lg[:], o, v("bg", 0, EXPERTS)[:, None, :].to_broadcast(
                                [P, NT, EXPERTS]), ALU.add).then_inc(s["lg"], 1)
                            dve.wait_ge(s["lg"], 1)
                            for j in range(NT):
                                nc.vector.max(top[:, j, :], lg[:, j, :]).then_inc(s["top"], 1)
                            dve.wait_ge(s["top"], NT)
                            for j in range(NT):
                                nc.vector.max_index(idx[:, j, :], top[:, j, :], lg[:, j, :]).then_inc(s["idx"], 1)
                            nc.vector.tensor_tensor(gap[:, :, 0:1], top[:, :, 0:1], top[:, :, 1:2],
                                                    ALU.subtract).then_inc(s["gap"], 1)
                            dve.wait_ge(s["idx"], NT)
                            nc.vector.tensor_copy(idf[:], idx[:]).then_inc(s["one"], 1)
                            dve.wait_ge(s["one"], 1)
                            for i in range(2):
                                nc.vector.tensor_tensor(oh[:, i, :, :], iota_e[:, None, :].to_broadcast([P, NT, EXPERTS]),
                                                        idf[:, :, i:i + 1].to_broadcast([P, NT, EXPERTS]),
                                                        ALU.is_equal).then_inc(s["one"], 1)
                        elif stage == ("route", 2):
                            dve.wait_ge(s["tg"], 1)
                            nc.vector.tensor_scalar(gap[:, :, 1:2], gap[:, :, 0:1], -0.5, 0.5, ALU.mult,
                                                    ALU.add).then_inc(s["wts"], 1)
                            dve.wait_ge(s["wts"], 1)
                            nc.vector.tensor_scalar(gap[:, :, 0:1], gap[:, :, 0:1], 0.5, 0.5, ALU.mult,
                                                    ALU.add).then_inc(s["wts"], 1)
                            dve.wait_ge(s["wts"], 2)
                            dve.wait_ge(s["one"], 3)
                            for i in range(2):
                                nc.vector.tensor_tensor(oh[:, i, :, :], oh[:, i, :, :],
                                                        gap[:, :, i:i + 1].to_broadcast([P, NT, EXPERTS]),
                                                        ALU.mult).then_inc(s["one"], 1)
                            dve.wait_ge(s["one"], 5)
                            nc.vector.tensor_tensor(g_tok[:, :, 0:EXPERTS], oh[:, 0, :, :], oh[:, 1, :, :],
                                                    ALU.add).then_inc(s["g_split"], 1)
                            split(g_tok, g_hi, EXPERTS, SPLIT, s["g_split"])
                        elif kind == "expert":
                            h, m = stage[1:]
                            o = full(dve, ("exp_g", h, m))
                            dve.wait_ge(s["exp_g"], NM * h + m + 1)
                            nc.vector.tensor_tensor(weighed[h][:, m, :], o[:], weighed[h][:, m, :],
                                                    ALU.mult).then_inc(s["gx"], 1)

                    def mixer_end(d, h):
                        dve.wait_ge(s["z"], 4)
                        o = full(dve, ("y_t", d, h))
                        nc.vector.scalar_tensor_tensor(out=half(ycm[:, d, :], h), in0=half(u[:, d, :], h),
                                                       scalar=v("d", d), in1=o[:], op0=ALU.mult,
                                                       op1=ALU.add).then_inc(s["y_sum"], 1)
                        dve.wait_ge(s["y_sum"], 2 * d + h + 1)
                        nc.vector.tensor_tensor(half(ycm[:, d, :], h), half(ycm[:, d, :], h), half(zs[:, d, :], h),
                                                ALU.mult).then_inc(s["y"], 1)

                    for slot, k in SLOTS:
                        if do_scan:
                            if slot == "in":
                                mixer_in(k)
                            elif slot == "scan":
                                scan(k)
                            else:
                                mixer_end(k // 2, k % 2)
                        for stage in plan["V", (slot, k)]:
                            rest(stage)

            nc.gpsimd.sem_clear(clear)
            nc.all_engine_barrier(sem_only=True)

        body(True, False, True, 0)
        with nc.Fori(1, BATCH - 1) as b:
            body(True, True, True, b)
        body(True, True, False, BATCH - 1)
        body(False, True, False, BATCH)


def kernel(**inputs):
    import numpy as np
    import concourse.bacc as bacc
    from concourse.bass_utils import run_bass_kernel_spmd

    a = {k: np.asarray(t) for k, t in inputs.items()}

    def rows_to(t):
        n = t.shape[0] // P
        return np.ascontiguousarray(t.reshape(n, P, -1).transpose(1, 0, 2).reshape(P, -1))

    wx = a["L0_attn_W_x"]
    gate = a["L1_attn_W_gate"]
    spread = lambda t: np.repeat(t, P // HEADS, axis=0)
    wts = np.concatenate([
        a["L0_attn_W_in"].T, rows_to(wx[DI:].T), rows_to(a["L0_attn_W_out"].T), a["L0_ffn_w1_w"].T,
        a["L0_ffn_w2_w"].T, rows_to(a["L0_ffn_h1_w"].T), rows_to(a["L0_ffn_h2_w"].T), rows_to(a["L0_ffn_w3_w"].T),
        a["L1_attn_W_in"].T, spread(gate[:HEADS]).T, spread(gate[HEADS:]).T, a["L1_attn_W_out"].T,
        a["L1_ffn_W1"].reshape(EXPERTS * RANK, P).T, rows_to(a["L1_ffn_W2"].transpose(0, 2, 1).reshape(-1, P)),
        a["L1_ffn_Wg"].T], axis=1)
    col = lambda t: rows_to(t.reshape(-1, 1))
    vecs = np.concatenate([
        rows_to(a["L0_attn_conv_w"].reshape(DI, TAPS)), col(a["L0_attn_conv_b"]), col(a["L0_attn_b_dt"]),
        rows_to(a["L0_attn_A_log"]), col(a["L0_attn_D"]), col(a["L0_attn_ln_g"]), col(a["L0_attn_ln_b"]),
        col(a["L0_ffn_w1_s"]), col(a["L0_ffn_w2_s"]), col(a["L0_ffn_h1_s"]), col(a["L0_ffn_h2_s"]),
        col(a["L0_ffn_w3_s"]), col(a["L1_attn_ln_g"]), col(a["L1_attn_ln_b"]),
        col(spread(a["L1_attn_b_gate"][:HEADS])), col(spread(a["L1_attn_b_gate"][HEADS:])),
        col(spread(a["L1_attn_eig_raw"])), np.broadcast_to(a["L1_ffn_bg"], (P, EXPERTS))], axis=1)
    pre = np.concatenate([rows_to(wx[:DI]), rows_to(a["L0_attn_W_dt"].T)], axis=1)
    cmod = np.concatenate([a["L0_c"].T, a["L1_c"].T], axis=1)
    wmod = np.concatenate([a["L0_wmod"], a["L1_wmod"]], axis=1)
    arrays = {"in_x": a["L0_attn_x"], "in_wts": wts, "in_vecs": vecs, "in_pre": pre, "in_cmod": cmod, "in_wmod": wmod}
    arrays = {k: np.ascontiguousarray(t) for k, t in arrays.items()}

    nc = bacc.Bacc("TRN2", target_bir_lowering=False, num_devices=1)
    args = [nc.dram_tensor(k, t.shape, mybir.dt.from_np(t.dtype), kind="ExternalInput").ap() for k, t in arrays.items()]
    args.append(nc.dram_tensor("out_0", (BATCH, L, P), F32, kind="ExternalOutput").ap())
    build(nc, *args)
    r = run_bass_kernel_spmd(nc, [arrays], core_ids=[0])
    return r.results[0]["out_0"]
```
